# Optimizing a Trainium2 kernel written in Bass

```python
import numpy as np
import jax
import jax.numpy as jnp

def _softmax(x, axis=-1):
    return jax.nn.softmax(x, axis=axis)

def _gelu(x):
    return jax.nn.gelu(x, approximate=True)

def _silu(x):
    return jax.nn.silu(x)

def _sigmoid(x):
    return jax.nn.sigmoid(x)

def _layernorm(x, axis=-1, eps=1e-05):
    m = jnp.mean(x, axis=axis, keepdims=True)
    v = jnp.var(x, axis=axis, keepdims=True)
    return (x - m) / jnp.sqrt(v + eps)

def _scatter_add(tgt, idx, src, axis=0):
    return tgt.at[idx].add(src)

def _segment_sum(src, seg, n):
    return jax.ops.segment_sum(src, seg, n)
kernel_name = 'mk_macaron_d1_jaxref_r4_b3d023'

def setup_inputs(seed: int=0):
    np.random.seed(seed)
    _w = jnp.asarray

    def _L0_attn_setup():
        import jax, jax.numpy as jnp
        import numpy as np
        DIM = 256
        N_QUAT = DIM // 4
        LN_EPS = 1e-05
        NORM_EPS = 1e-12

        def quat_mul(q1, q2):
            r1, i1, j1, k1 = (q1[..., 0], q1[..., 1], q1[..., 2], q1[..., 3])
            r2, i2, j2, k2 = (q2[..., 0], q2[..., 1], q2[..., 2], q2[..., 3])
            r = r1 * r2 - i1 * i2 - j1 * j2 - k1 * k2
            i = r1 * i2 + i1 * r2 + j1 * k2 - k1 * j2
            j = r1 * j2 - i1 * k2 + j1 * r2 + k1 * i2
            k = r1 * k2 + i1 * j2 - j1 * i2 + k1 * r2
            return jnp.stack([r, i, j, k], axis=-1)

        def quat_conj(q):
            return q * jnp.array([1.0, -1.0, -1.0, -1.0], dtype=q.dtype)
        key = jax.random.key(seed)
        ks = jax.random.split(key, 7)
        B, L, D = (4, 1024, DIM)
        s = 1.0 / np.sqrt(D)
        return {'x': jax.random.normal(ks[0], (B, L, D), dtype=jnp.float32), 'Wk': jax.random.normal(ks[1], (D, D), dtype=jnp.float32) * s, 'bk': jnp.zeros((D,), dtype=jnp.float32), 'Wv': jax.random.normal(ks[2], (D, D), dtype=jnp.float32) * s, 'bv': jnp.zeros((D,), dtype=jnp.float32), 'ln_g': jnp.ones((D,), dtype=jnp.float32), 'ln_b': jnp.zeros((D,), dtype=jnp.float32), 'Wo': jax.random.normal(ks[3], (D, D), dtype=jnp.float32) * s, 'bo': jnp.zeros((D,), dtype=jnp.float32)}
    _L0_attn_in = _L0_attn_setup()

    def _L0_ffn_setup():
        import jax, jax.numpy as jnp
        import numpy as np
        DIM = 256

        def _reference_tuple_inner(x, W_r, W_k, W_v, mu_r, mu_k):
            B, T, C = x.shape
            x_prev = jnp.concatenate([jnp.zeros((B, 1, C), x.dtype), x[:, :-1, :]], axis=1)
            xr = mu_r * x + (1.0 - mu_r) * x_prev
            xk = mu_k * x + (1.0 - mu_k) * x_prev
            r = jax.nn.sigmoid(jnp.einsum('btc,dc->btd', xr, W_r))
            k = jnp.einsum('btc,dc->btd', xk, W_k)
            k_act = jnp.square(jax.nn.relu(k))
            out = r * jnp.einsum('btc,dc->btd', k_act, W_v)
            new_state = x[:, -1, :]
            return (out, new_state)
        key = jax.random.key(seed)
        ks = jax.random.split(key, 6)
        B, T, C = (8, 512, DIM)
        x = jax.random.normal(ks[0], (B, T, C), dtype=jnp.float32)
        s = 1.0 / np.sqrt(C)
        W_r = jax.random.uniform(ks[1], (C, C), jnp.float32, -s, s)
        W_k = jax.random.uniform(ks[2], (C, C), jnp.float32, -s, s)
        W_v = jax.random.uniform(ks[3], (C, C), jnp.float32, -s, s)
        mu_r = jax.random.uniform(ks[4], (C,), jnp.float32)
        mu_k = jax.random.uniform(ks[5], (C,), jnp.float32)
        return {'x': x, 'W_r': W_r, 'W_k': W_k, 'W_v': W_v, 'mu_r': mu_r, 'mu_k': mu_k}
    _L0_ffn_in = _L0_ffn_setup()
    _d = {'L0_attn_x': _L0_attn_in['x'], 'L0_attn_Wk': _L0_attn_in['Wk'], 'L0_attn_bk': _L0_attn_in['bk'], 'L0_attn_Wv': _L0_attn_in['Wv'], 'L0_attn_bv': _L0_attn_in['bv'], 'L0_attn_ln_g': _L0_attn_in['ln_g'], 'L0_attn_ln_b': _L0_attn_in['ln_b'], 'L0_attn_Wo': _L0_attn_in['Wo'], 'L0_attn_bo': _L0_attn_in['bo'], 'L0_ffn_W_r': _L0_ffn_in['W_r'], 'L0_ffn_W_k': _L0_ffn_in['W_k'], 'L0_ffn_W_v': _L0_ffn_in['W_v'], 'L0_ffn_mu_r': _L0_ffn_in['mu_r'], 'L0_ffn_mu_k': _L0_ffn_in['mu_k']}
    _x0 = _d['L0_attn_x']
    _d['L0_attn_x'] = jax.random.normal(jax.random.fold_in(jax.random.key(seed), 1), (2, 4096, 256), dtype=_x0.dtype)
    del _x0
    return _d

def reference(L0_attn_x, L0_attn_Wk, L0_attn_bk, L0_attn_Wv, L0_attn_bv, L0_attn_ln_g, L0_attn_ln_b, L0_attn_Wo, L0_attn_bo, L0_ffn_W_r, L0_ffn_W_k, L0_ffn_W_v, L0_ffn_mu_r, L0_ffn_mu_k):

    def _L0_attn_ref(x, Wk, bk, Wv, bv, ln_g, ln_b, Wo, bo):
        import jax, jax.numpy as jnp
        import numpy as np
        DIM = 256
        N_QUAT = DIM // 4
        LN_EPS = 1e-05
        NORM_EPS = 1e-12

        def quat_mul(q1, q2):
            r1, i1, j1, k1 = (q1[..., 0], q1[..., 1], q1[..., 2], q1[..., 3])
            r2, i2, j2, k2 = (q2[..., 0], q2[..., 1], q2[..., 2], q2[..., 3])
            r = r1 * r2 - i1 * i2 - j1 * j2 - k1 * k2
            i = r1 * i2 + i1 * r2 + j1 * k2 - k1 * j2
            j = r1 * j2 - i1 * k2 + j1 * r2 + k1 * i2
            k = r1 * k2 + i1 * j2 - j1 * i2 + k1 * r2
            return jnp.stack([r, i, j, k], axis=-1)

        def quat_conj(q):
            return q * jnp.array([1.0, -1.0, -1.0, -1.0], dtype=q.dtype)
        B, L, D = x.shape
        keys = (x @ Wk.T + bk).reshape(B, L, N_QUAT, 4)
        knorm = jnp.linalg.norm(keys, axis=-1, keepdims=True)
        keys = keys / jnp.maximum(knorm, NORM_EPS)
        values = (x @ Wv.T + bv).reshape(B, L, N_QUAT, 4)
        bound = quat_mul(values, keys)
        memory = jnp.cumsum(bound, axis=1)
        retrieved = quat_mul(memory, quat_conj(keys)).reshape(B, L, D)
        positions = jnp.arange(1, L + 1, dtype=x.dtype)
        retrieved = retrieved / jnp.sqrt(positions)[None, :, None]
        mu = jnp.mean(retrieved, axis=-1, keepdims=True)
        var = jnp.var(retrieved, axis=-1, keepdims=True)
        normed = (retrieved - mu) / jnp.sqrt(var + LN_EPS) * ln_g + ln_b
        return x + (normed @ Wo.T + bo)

    def _L0_ffn_ref(x, W_r, W_k, W_v, mu_r, mu_k):
        import jax, jax.numpy as jnp
        import numpy as np
        DIM = 256

        def _reference_tuple_inner(x, W_r, W_k, W_v, mu_r, mu_k):
            B, T, C = x.shape
            x_prev = jnp.concatenate([jnp.zeros((B, 1, C), x.dtype), x[:, :-1, :]], axis=1)
            xr = mu_r * x + (1.0 - mu_r) * x_prev
            xk = mu_k * x + (1.0 - mu_k) * x_prev
            r = jax.nn.sigmoid(jnp.einsum('btc,dc->btd', xr, W_r))
            k = jnp.einsum('btc,dc->btd', xk, W_k)
            k_act = jnp.square(jax.nn.relu(k))
            out = r * jnp.einsum('btc,dc->btd', k_act, W_v)
            new_state = x[:, -1, :]
            return (out, new_state)
        return _reference_tuple_inner(x, W_r, W_k, W_v, mu_r, mu_k)[0]
    x = L0_attn_x
    x = x + 0.5 * _L0_ffn_ref(_layernorm(x, axis=-1), L0_ffn_W_r, L0_ffn_W_k, L0_ffn_W_v, L0_ffn_mu_r, L0_ffn_mu_k)
    x = x + _L0_attn_ref(_layernorm(x, axis=-1), L0_attn_Wk, L0_attn_bk, L0_attn_Wv, L0_attn_bv, L0_attn_ln_g, L0_attn_ln_b, L0_attn_Wo, L0_attn_bo)
    x = x + 0.5 * _L0_ffn_ref(_layernorm(x, axis=-1), L0_ffn_W_r, L0_ffn_W_k, L0_ffn_W_v, L0_ffn_mu_r, L0_ffn_mu_k)
    return x

_drawn_inputs = setup_inputs


def setup_inputs(seed=0):
    import zlib

    import numpy as np

    out = dict(_drawn_inputs(seed))
    spreads = {'L0_attn_bk': (0.0, 0.1),
     'L0_attn_bv': (0.0, 0.1),
     'L0_attn_ln_g': (1.0, 0.2),
     'L0_attn_ln_b': (0.0, 0.1),
     'L0_attn_bo': (0.0, 0.1)}
    factors = {'L0_ffn_W_r': 4.445, 'L0_ffn_mu_r': 8.0}
    for name, (base, spread) in spreads.items():
        noise = np.random.default_rng([zlib.crc32(name.encode()), seed]).standard_normal(out[name].shape)
        drawn = base * np.exp(spread * noise) if base else spread * noise
        out[name] = jnp.asarray(drawn.astype(out[name].dtype))
    for name, factor in factors.items():
        out[name] = (out[name] * factor).astype(out[name].dtype)
    return out
```

```python
from contextlib import ExitStack

import concourse.bass as bass
from concourse import mybir

F32 = mybir.dt.float32
BF16 = mybir.dt.bfloat16
I32 = mybir.dt.int32
ALU = mybir.AluOpType
ACT = mybir.ActivationFunctionType

P = 128
LN_EPS = 1e-5
NORM_EPS = 1e-12
STAT = 6


def need(engine, semaphore, count):
    if isinstance(count, int) and count <= 0:
        return
    engine.wait_ge(semaphore, count)


def rounds(engine, n, body):
    body(0, True, False)
    with engine.Fori(1, n - 1) as j:
        body(j, False, False)
    body(n - 1, False, True)


def macaron(nc, x, w_kv, w_o, w_r, w_k, w_v, b_kv, b_o, columns, out):
    B, L, D = x.shape
    FC = D // P
    NT = L // P
    Q = D // 4
    CT = 4
    CW = CT * P
    NJ = NT // CT
    NP = NT // 2
    NS = B * NJ
    MS = B * NP
    assert B == 2 and D == 2 * P and L % CW == 0

    with ExitStack() as ctx:
        def sb(name, shape, dt=F32):
            return ctx.enter_context(nc.sbuf_tensor(name, shape, dt))

        def sem(name):
            return ctx.enter_context(nc.semaphore(name))

        res = sb("res", [P, B * NT * D])
        wkv = sb("wkv", [P, FC, 2 * D])
        wo = sb("wo", [P, FC, D])
        wr = sb("wr", [P, FC, D])
        wk = sb("wk", [P, FC, D])
        wv = sb("wv", [P, FC, D])
        cols = sb("cols", [P, 4 * FC])
        mur, muk, lng, lnb = (cols[:, i * FC:(i + 1) * FC] for i in range(4))
        lnb_rows = sb("lnb_rows", [P, FC, P])
        bias = sb("bias", [P, 3 * D])
        bias_rest = sb("bias_rest", [P, 3 * D])
        bias_mid = sb("bias_mid", [P, 3 * D], BF16)
        bias_part = sb("bias_part", [P, 3 * D], BF16)
        bias3 = sb("bias3", [P, 3 * D], BF16)
        ones = sb("ones", [P, P], BF16)
        ident = sb("ident", [P, P])
        upto = sb("upto", [P, P])
        after = sb("after", [P, P])
        zeros = sb("zeros", [P, D])
        pos = sb("pos", [P, NT], I32)
        epspos = sb("epspos", [P, NT])
        minus_half = sb("minus_half", [P, CT])
        spare = sb("spare", [P, 1])
        eps_tile = sb("eps_tile", [P, CT])

        st = sb("st", [P, 2, CT, STAT])
        mv = sb("mv", [P, 2, CT, 2])
        rstd = sb("rstd", [P, 2, CT])
        xn = sb("xn", [P, 2, CT, D])
        xnT = sb("xnT", [P, 2, FC, CW + 1])
        diff = sb("diff", [P, FC, CW])
        xr = sb("xr", [P, 2, FC, CW])
        xk = sb("xk", [P, 2, FC, CW])
        relu_k = sb("relu_k", [P, FC, CW])
        kact = sb("kact", [P, FC, CW])
        gate = sb("gate", [P, CT, D])
        gated = sb("gated", [P, CT, D])

        m_xn = sb("m_xn", [P, 2, D])
        m_xnT = sb("m_xnT", [P, FC, 2 * P])
        ksq = sb("ksq", [P, 2, D])
        ksum = sb("ksum", [P, 2, 2 * Q])
        knorm = sb("knorm", [P, 2, Q])
        kinv = sb("kinv", [P, 2, Q])
        khat = sb("khat", [P, 2, D])
        prod = sb("prod", [P, 2, 16, Q])
        half_a = sb("half_a", [P, 2, 4, Q])
        half_q = sb("half_q", [P, 2, 4, Q])
        bound = sb("bound", [P, 2, D])
        ret = sb("ret", [P, 2, 2, D])
        r_st = sb("r_st", [P, 2, 2, STAT])
        r_mv = sb("r_mv", [P, 2, 2, 2])
        r_var = sb("r_var", [P, 2, 2])
        r_rstd = sb("r_rstd", [P, 2, 2])
        r_shift = sb("r_shift", [P, 2, 2])
        r_shift_a = sb("r_shift_a", [P, 2, 2])
        normed = sb("normed", [P, 2, D])
        normedT = sb("normedT", [P, FC, 2 * P])

        bank = [ctx.enter_context(nc.psum_tensor(f"bank{i}", [P, 2, 512], F32)) for i in range(4)]
        xT_ps, k_ps, r_ps, v_ps = (t[:, :, :] for t in bank)
        r_tok = r_ps.rearrange("p h (t n) -> p (h t) n", n=D)
        v_tok = v_ps.rearrange("p h (t n) -> p (h t) n", n=D)
        t_bank = bank[0][:, 0, :].rearrange("p (f t) -> p f t", f=FC)
        o_bank = bank[0][:, 1, :].rearrange("p (t n) -> p t n", t=2)
        keys = [bank[1][:, b, :].rearrange("p (t n) -> p t n", t=2) for b in range(2)]
        values = [bank[2][:, b, :].rearrange("p (t n) -> p t n", t=2) for b in range(2)]
        memory = [bank[3][:, b, 0:D] for b in range(2)]

        def tiles(tile, n):
            return res[:, bass.ds(tile * D, n * D)].rearrange("p (t n) -> p t n", n=D)

        def rows(dram, b, j, n):
            return dram[b, bass.ds(j * (n * P), n * P), :].rearrange("(t p) n -> p t n", p=P)

        consts_in = sem("consts_in")
        consts_pool = sem("consts_pool")
        setup = sem("setup")
        lnb_folded = sem("lnb_folded")
        consts_ready = sem("consts_ready")
        x_in = [sem(f"x_in{b}") for b in range(2)]
        x_out = [sem(f"x_out{b}") for b in range(2)]

        shift_zeroed = sem("shift_zeroed")
        FFN_SEMS = ["st_done", "stats_done", "var_done", "rstd_done", "xn_done", "T_done", "carry_done", "xnT_done",
                    "diff_done", "xk_done", "xr_done", "k_done", "relu_done", "kact_done", "r_done", "gate_done", "v_done",
                    "gated_done", "res_done"]
        ffn_sems = [{n: sem(f"f{i}_{n}") for n in FFN_SEMS} for i in range(2)]
        MEM_SEMS = ["st_done", "stats_done", "var_done", "rstd_done", "xn_done", "T_done", "xnT_done", "res_done",
                    "K_done", "V_done", "ksq_done", "khalf_done", "ksum_done", "knorm_done", "kmax_done", "kinv_done",
                    "khat_done", "rst_done", "rstats_done", "rvar_done", "rrstd_done", "shift_done", "normed_done", "nT_done",
                    "normedT_done", "O_done", "x_done"]
        m = {n: sem(f"m_{n}") for n in MEM_SEMS}
        bprod_done = [sem(f"m_bprod{i}_done") for i in range(2)]
        bhalf_done = [sem(f"m_bhalf{i}_done") for i in range(2)]
        bound_done = [sem(f"m_bound{i}_done") for i in range(2)]
        upto_done = [sem(f"m_upto{i}_done") for i in range(2)]
        after_done = [sem(f"m_after{i}_done") for i in range(2)]
        rprod_done = [sem(f"m_rprod{i}_done") for i in range(2)]
        rhalf_done = [sem(f"m_rhalf{i}_done") for i in range(2)]
        ret_done = [sem(f"m_ret{i}_done") for i in range(2)]

        def x_ready(engine, stage, b, j):
            if stage == 0:
                engine.wait_ge(x_in[b], 16 * (j + 1))
            else:
                engine.wait_ge(m["x_done"], MS)

        block = ctx.enter_context(nc.Block())

        @block.sync
        def _(sp):
            loads = [(wk[:, :, :], w_k.rearrange("(f p) n -> p f n", p=P)),
                     (wr[:, :, :], w_r.rearrange("(f p) n -> p f n", p=P)),
                     (wv[:, :, :], w_v.rearrange("(f p) n -> p f n", p=P)),
                     (cols[:, :], columns),
                     (wkv[:, :, :], w_kv.rearrange("(f p) n -> p f n", p=P)),
                     (wo[:, :, :], w_o.rearrange("(f p) n -> p f n", p=P)),
                     (bias[:, 0:2 * D], b_kv.partition_broadcast(P)),
                     (bias[:, 2 * D:], b_o.partition_broadcast(P))]
            for b in range(2):
                sp.dma_start(tiles(b * NT, CT), rows(x, b, 0, CT)).then_inc(x_in[b], 16)
            for dst, src in loads:
                sp.dma_start(dst, src).then_inc(consts_in, 16)
            assert len(loads) == CONST_LOADS
            with sp.Fori(1, NJ) as j:
                for b in range(2):
                    sp.wait_ge(x_in[b], 16 * j)
                    sp.dma_start(tiles(b * NT + j * CT, CT), rows(x, b, j, CT)).then_inc(x_in[b], 16)
            done = ffn_sems[1]["res_done"]
            with sp.Fori(0, NJ) as j:
                for b in range(2):
                    sp.wait_ge(done, 2 * j + b + 1)
                    sp.dma_start(rows(out, b, j, CT), tiles(b * NT + j * CT, CT)).then_inc(x_out[b], 16)
            for b in range(2):
                sp.wait_ge(x_out[b], 16 * NJ)

        @block.vector
        def _(dve):
            def prepare():
                dve.wait_ge(consts_in, 16 * CONST_LOADS)
                n = 0

                def own(instruction):
                    nonlocal n
                    n += 1
                    instruction.then_inc(setup, 1)
                    dve.wait_ge(setup, n)

                nc.vector.tensor_scalar(wv[:, :, :], wv[:, :, :], 0.5, None, ALU.mult)
                own(nc.vector.tensor_copy(lnb_rows[:, :, :], lnb[:, :].unsqueeze(2).to_broadcast([P, FC, P])))
                own(nc.vector.memset(bias3[:, :], 0.0))
                nc.vector.memset(ones[:, :], 1.0).then_inc(lnb_folded, 1)
                dve.wait_ge(lnb_folded, 2)
                own(nc.vector.tensor_tensor(bias[:, 2 * D:], o_bank[:, 0, :], bias[:, 2 * D:], ALU.add))
                for f in range(FC):
                    nc.vector.tensor_scalar(wo[:, f, :], wo[:, f, :], lng[:, f:f + 1], None, ALU.mult)
                own(nc.vector.tensor_copy(bias_part[:, :], bias[:, :]))
                nc.vector.tensor_copy(bias3[0:1, :], bias_part[0:1, :])
                own(nc.vector.tensor_tensor(bias_rest[:, :], bias[:, :], bias_part[:, :], ALU.subtract))
                own(nc.vector.tensor_copy(bias_mid[:, :], bias_rest[:, :]))
                nc.vector.tensor_copy(bias3[32:33, :], bias_mid[32:33, :])
                own(nc.vector.tensor_tensor(bias_rest[:, :], bias_rest[:, :], bias_mid[:, :], ALU.subtract))
                own(nc.vector.tensor_copy(bias3[64:65, :], bias_rest[64:65, :]))
                dve.wait_ge(consts_pool, POOL_CONSTS)
                nc.vector.tensor_scalar(epspos[:, :], pos[:, :], LN_EPS, None, ALU.mult).then_inc(consts_ready, 1)

            prepare()

            def own_wait(semaphore, count):
                dve.wait_ge(semaphore, count)
                nc.vector.memset(spare[:, :], 0.0)

            def ffn(stage):
                e = ffn_sems[stage]

                def stats(j, b):
                    s = 2 * j + b
                    x_ready(dve, stage, b, j)
                    t = tiles(b * NT + j * CT, CT)
                    for i in range(CT):
                        last = nc.vector.bn_stats(st[:, b, i, :], t[:, i, :])
                    last.then_inc(e["st_done"], 1)
                    own_wait(e["st_done"], s + 1)
                    for i in range(CT):
                        last = nc.vector.bn_aggr(mv[:, b, i, :], st[:, b, i, :])
                    last.then_inc(e["stats_done"], 1)

                def normalize(j, b):
                    s = 2 * j + b
                    dve.wait_ge(e["rstd_done"], s + 1)
                    need(dve, e["T_done"], s - 1)
                    t = tiles(b * NT + j * CT, CT)
                    for i in range(CT):
                        last = nc.vector.tensor_scalar(xn[:, b, i, :], t[:, i, :], mv[:, b, i, 0:1], rstd[:, b, i:i + 1],
                                                       ALU.subtract, ALU.mult)
                    last.then_inc(e["xn_done"], 1)

                def mix(j, b):
                    s = 2 * j + b
                    dve.wait_ge(e["xnT_done"], s + 1)
                    need(dve, e["r_done"], s - 1)
                    nc.vector.tensor_tensor(diff[:, :, :], xnT[:, b, :, 1:CW + 1], xnT[:, b, :, 0:CW],
                                            ALU.subtract).then_inc(e["diff_done"], 1)
                    dve.wait_ge(e["diff_done"], s + 1)
                    for f in range(FC):
                        last = nc.vector.scalar_tensor_tensor(xk[:, b, f, :], diff[:, f, :], muk[:, f:f + 1],
                                                              xnT[:, b, f, 0:CW], ALU.mult, ALU.add)
                    last.then_inc(e["xk_done"], 1)
                    for f in range(FC):
                        last = nc.vector.scalar_tensor_tensor(xr[:, b, f, :], diff[:, f, :], mur[:, f:f + 1],
                                                              xnT[:, b, f, 0:CW], ALU.mult, ALU.add)
                    last.then_inc(e["xr_done"], 1)

                def gating(j, b):
                    s = 2 * j + b
                    dve.wait_ge(e["gate_done"], s + 1)
                    dve.wait_ge(e["v_done"], s + 1)
                    need(dve, e["res_done"], s)
                    nc.vector.tensor_tensor(gated[:, :, :], v_tok, gate[:, :, :], ALU.mult).then_inc(e["gated_done"], 1)

                stats(0, 0)
                stats(0, 1)
                normalize(0, 0)
                mix(0, 0)

                def body(j, first, last):
                    for b in range(2):
                        nj, nb = (j, 1) if b == 0 else (j + 1, 0)
                        ahead = not (last and b == 1)
                        if ahead:
                            normalize(nj, nb)
                        if not last:
                            stats(j + 1, b)
                        if ahead:
                            mix(nj, nb)
                        gating(j, b)

                rounds(dve, NJ, body)

            def mem():
                def stats(j, b):
                    s = 2 * j + b
                    dve.wait_ge(ffn_sems[0]["res_done"], NS)
                    need(dve, m["xn_done"], s - 1)
                    t = tiles(b * NT + j * 2, 2)
                    for i in range(2):
                        last = nc.vector.bn_stats(st[:, b, i, :], t[:, i, :])
                    last.then_inc(m["st_done"], 1)
                    own_wait(m["st_done"], s + 1)
                    for i in range(2):
                        last = nc.vector.bn_aggr(mv[:, b, i, :], st[:, b, i, :])
                    last.then_inc(m["stats_done"], 1)

                def key_inverse(j, b):
                    s = 2 * j + b
                    dve.wait_ge(m["knorm_done"], s + 1)
                    need(dve, m["khat_done"], s)
                    nc.vector.tensor_scalar(knorm[:, :, :], knorm[:, :, :], NORM_EPS, None, ALU.max).then_inc(m["kmax_done"], 1)
                    dve.wait_ge(m["kmax_done"], s + 1)
                    nc.vector.reciprocal(kinv[:, :, :], knorm[:, :, :]).then_inc(m["kinv_done"], 1)

                def key_unit(j, b):
                    s = 2 * j + b
                    dve.wait_ge(m["kinv_done"], s + 1)
                    dve.wait_ge(m["K_done"], s + 1)
                    dve.wait_ge(m["ksq_done"], s + 1)
                    need(dve, rprod_done[1], s)
                    nc.vector.tensor_tensor(khat[:, :, :].rearrange("p t (c n) -> p t c n", n=Q),
                                            keys[b].rearrange("p t (c n) -> p t c n", n=Q),
                                            kinv[:, :, :].unsqueeze(2).to_broadcast([P, 2, 4, Q]), ALU.mult).then_inc(m["khat_done"], 1)

                def all_products(i, of, done):
                    nc.vector.tensor_tensor(
                        prod[:, i, :, :].rearrange("p (a b) n -> p a b n", a=4),
                        of.rearrange("p (a n) -> p a n", n=Q).unsqueeze(2).to_broadcast([P, 4, 4, Q]),
                        khat[:, i, :].rearrange("p (b n) -> p b n", n=Q).unsqueeze(1).to_broadcast([P, 4, 4, Q]),
                        ALU.mult).then_inc(done, 1)

                def bind(j, b, i):
                    s = 2 * j + b
                    dve.wait_ge(m["khat_done"], s + 1)
                    dve.wait_ge(m["V_done"], s + 1)
                    need(dve, ret_done[i], s)
                    all_products(i, values[b][:, i, :], bprod_done[i])

                def retrieve(j, b, i):
                    s = 2 * j + b
                    dve.wait_ge(upto_done[i], s + 1)
                    all_products(i, memory[b], rprod_done[i])

                def ret_stats(j, b):
                    s = 2 * j + b
                    for i in range(2):
                        dve.wait_ge(ret_done[i], s + 1)
                    need(dve, m["normed_done"], s - 1)
                    for i in range(2):
                        last = nc.vector.bn_stats(r_st[:, b, i, :], ret[:, b, i, :])
                    last.then_inc(m["rst_done"], 1)
                    own_wait(m["rst_done"], s + 1)
                    for i in range(2):
                        last = nc.vector.bn_aggr(r_mv[:, b, i, :], r_st[:, b, i, :])
                    last.then_inc(m["rstats_done"], 1)

                def residual(j, b):
                    s = 2 * j + b
                    dve.wait_ge(m["O_done"], s + 1)
                    dve.wait_ge(m["res_done"], s + 1)
                    t = tiles(b * NT + j * 2, 2)
                    nc.vector.tensor_tensor(t, o_bank, t, ALU.add).then_inc(m["x_done"], 1)

                stats(0, 0)
                stats(0, 1)
                key_inverse(0, 0)

                def body(j, first, last):
                    for b in range(2):
                        nj, nb = (j, 1) if b == 0 else (j + 1, 0)
                        pj, pb = (j, 0) if b == 1 else (j - 1, 1)
                        behind = not (first and b == 0)
                        key_unit(j, b)
                        bind(j, b, 0)
                        bind(j, b, 1)
                        if behind:
                            ret_stats(pj, pb)
                        if not last:
                            stats(j + 1, b)
                        retrieve(j, b, 0)
                        if not (last and b == 1):
                            key_inverse(nj, nb)
                        retrieve(j, b, 1)
                        if behind:
                            residual(pj, pb)

                rounds(dve, NP, body)
                ret_stats(NP - 1, 1)
                residual(NP - 1, 1)

            ffn(0)
            mem()
            ffn(1)

        @block.scalar
        def _(act):
            def ffn(stage):
                e = ffn_sems[stage]

                def evict_xT(j, b, first):
                    s = 2 * j + b
                    act.wait_ge(e["T_done"], s + 1)
                    need(act, e["xr_done"], s - 1)
                    if not first:
                        nc.scalar.copy(xnT[:, b, :, 0:1], xnT[:, b, :, CW:CW + 1]).then_inc(e["carry_done"], 1)
                        act.wait_ge(e["carry_done"], s - 1)
                    nc.scalar.copy(xnT[:, b, :, 1:CW + 1], xT_ps).then_inc(e["xnT_done"], 1)

                def relu(j, b):
                    s = 2 * j + b
                    act.wait_ge(e["k_done"], s + 1)
                    need(act, e["kact_done"], s)
                    nc.scalar.activation(relu_k[:, :, :], k_ps, ACT.Relu).then_inc(e["relu_done"], 1)

                def sigmoid(j, b):
                    s = 2 * j + b
                    act.wait_ge(e["r_done"], s + 1)
                    need(act, e["gated_done"], s)
                    nc.scalar.activation(gate[:, :, :], r_tok, ACT.Sigmoid).then_inc(e["gate_done"], 1)

                if stage == 0:
                    act.wait_ge(consts_pool, POOL_CONSTS)
                else:
                    act.wait_ge(shift_zeroed, 1)
                evict_xT(0, 0, True)

                def body(j, first, last):
                    for b in range(2):
                        relu(j, b)
                        if not (last and b == 1):
                            nj, nb = (j, 1) if b == 0 else (j + 1, 0)
                            evict_xT(nj, nb, first and b == 0)
                        sigmoid(j, b)

                rounds(act, NJ, body)

            def mem():
                def normalize(j, b):
                    s = 2 * j + b
                    act.wait_ge(m["rstd_done"], s + 1)
                    need(act, m["T_done"], s)
                    need(act, m["res_done"], s)
                    t = tiles(b * NT + j * 2, 2)
                    for i in range(2):
                        last = nc.scalar.activation(m_xn[:, i, :], t[:, i, :], ACT.Identity, bias=r_shift_a[:, b, i:i + 1],
                                                    scale=rstd[:, b, i:i + 1])
                    last.then_inc(m["xn_done"], 1)

                def evict_xT(j, b):
                    s = 2 * j + b
                    act.wait_ge(m["T_done"], s + 1)
                    need(act, m["V_done"], s)
                    nc.scalar.copy(m_xnT[:, :, :], t_bank).then_inc(m["xnT_done"], 1)

                def key_square(j, b):
                    s = 2 * j + b
                    act.wait_ge(m["K_done"], s + 1)
                    need(act, m["ksum_done"], s)
                    nc.scalar.activation(ksq[:, :, :], keys[b], ACT.Square).then_inc(m["ksq_done"], 1)

                def key_norm(j, b):
                    s = 2 * j + b
                    act.wait_ge(m["ksum_done"], s + 1)
                    need(act, m["kinv_done"], s)
                    nc.scalar.activation(knorm[:, :, :], ksum[:, :, 0:Q], ACT.Sqrt).then_inc(m["knorm_done"], 1)

                def ret_normalize(j, b):
                    s = 2 * j + b
                    act.wait_ge(m["rrstd_done"], s + 1)
                    need(act, m["nT_done"], s)
                    for i in range(2):
                        last = nc.scalar.activation(normed[:, i, :], ret[:, b, i, :], ACT.Identity, bias=r_shift[:, b, i:i + 1],
                                                    scale=r_rstd[:, b, i:i + 1])
                    last.then_inc(m["normed_done"], 1)

                def evict_nT(j, b):
                    s = 2 * j + b
                    act.wait_ge(m["nT_done"], s + 1)
                    need(act, m["O_done"], s)
                    nc.scalar.copy(normedT[:, :, :], t_bank).then_inc(m["normedT_done"], 1)

                normalize(0, 0)
                evict_xT(0, 0)
                key_square(0, 0)
                key_norm(0, 0)

                def body(j, first, last):
                    for b in range(2):
                        nj, nb = (j, 1) if b == 0 else (j + 1, 0)
                        pj, pb = (j, 0) if b == 1 else (j - 1, 1)
                        ahead, behind = not (last and b == 1), not (first and b == 0)
                        if ahead:
                            normalize(nj, nb)
                            evict_xT(nj, nb)
                            key_square(nj, nb)
                            key_norm(nj, nb)
                        if behind:
                            ret_normalize(pj, pb)
                            evict_nT(pj, pb)

                rounds(act, NP, body)
                ret_normalize(NP - 1, 1)
                evict_nT(NP - 1, 1)

            ffn(0)
            mem()
            ffn(1)

        @block.gpsimd
        def _(pool):
            def prepare():
                nc.gpsimd.memset(ident[:, :], 0.0)
                nc.gpsimd.memset(upto[:, :], 1.0)
                nc.gpsimd.memset(after[:, :], 1.0)
                nc.gpsimd.memset(zeros[:, :], 0.0)
                nc.gpsimd.memset(xnT[:, :, :, 0:1], 0.0)
                nc.gpsimd.memset(minus_half[:, :], -0.5)
                nc.gpsimd.memset(eps_tile[:, :], LN_EPS)
                nc.gpsimd.iota(pos[:, :], pattern=[[P, NT]], base=1, channel_multiplier=1).then_inc(consts_pool, 1)
                pool.wait_ge(consts_pool, 1)
                nc.gpsimd.affine_select(out=ident[:, :], in_=ident[:, :], compare_op=ALU.not_equal, fill=1.0,
                                        base=0, pattern=[[-1, P]], channel_multiplier=1)
                nc.gpsimd.affine_select(out=upto[:, :], in_=upto[:, :], compare_op=ALU.is_ge, fill=0.0,
                                        base=0, pattern=[[1, P]], channel_multiplier=-1)
                nc.gpsimd.affine_select(out=after[:, :], in_=after[:, :], compare_op=ALU.is_gt, fill=0.0,
                                        base=0, pattern=[[-1, P]], channel_multiplier=1).then_inc(consts_pool, 1)
                assert POOL_CONSTS == 2

            prepare()

            def ffn(stage):
                e = ffn_sems[stage]

                def inverse_std(j, b):
                    s = 2 * j + b
                    pool.wait_ge(e["stats_done"], s + 1)
                    need(pool, e["xn_done"], s - 1)
                    nc.gpsimd.tensor_tensor(rstd[:, b, :], mv[:, b, :, 1], eps_tile[:, :], ALU.add).then_inc(e["var_done"], 1)
                    pool.wait_ge(e["var_done"], s + 1)
                    nc.gpsimd.tensor_tensor(rstd[:, b, :], rstd[:, b, :], minus_half[:, :], ALU.pow).then_inc(e["rstd_done"], 1)

                def square(j, b):
                    s = 2 * j + b
                    pool.wait_ge(e["relu_done"], s + 1)
                    need(pool, e["v_done"], s)
                    nc.gpsimd.tensor_tensor(kact[:, :, :], relu_k[:, :, :], relu_k[:, :, :], ALU.mult).then_inc(e["kact_done"], 1)

                def residual(j, b):
                    s = 2 * j + b
                    pool.wait_ge(e["gated_done"], s + 1)
                    t = tiles(b * NT + j * CT, CT)
                    nc.gpsimd.tensor_tensor(t, t, gated[:, :, :], ALU.add).then_inc(e["res_done"], 1)

                inverse_std(0, 0)
                inverse_std(0, 1)

                def body(j, first, last):
                    for b in range(2):
                        if not last:
                            inverse_std(j + 1, b)
                        square(j, b)
                        residual(j, b)

                rounds(pool, NJ, body)

            def mem():
                def inverse_std(j, b):
                    s = 2 * j + b
                    pool.wait_ge(m["stats_done"], s + 1)
                    need(pool, m["xn_done"], s - 1)
                    nc.gpsimd.tensor_tensor(rstd[:, b, 0:2], mv[:, b, 0:2, 1], eps_tile[:, 0:2], ALU.add).then_inc(m["var_done"], 1)
                    pool.wait_ge(m["var_done"], 2 * s + 1)
                    nc.gpsimd.tensor_tensor(rstd[:, b, 0:2], rstd[:, b, 0:2], minus_half[:, 0:2], ALU.pow).then_inc(m["var_done"], 1)
                    pool.wait_ge(m["var_done"], 2 * s + 2)
                    nc.gpsimd.tensor_tensor(r_shift_a[:, b, :], mv[:, b, 0:2, 0], rstd[:, b, 0:2], ALU.mult).then_inc(m["shift_done"], 1)
                    pool.wait_ge(m["shift_done"], s + 1)
                    nc.gpsimd.tensor_tensor(r_shift_a[:, b, :], zeros[:, 0:2], r_shift_a[:, b, :], ALU.subtract).then_inc(m["rstd_done"], 1)

                def add_normalized(j, b):
                    s = 2 * j + b
                    pool.wait_ge(m["xn_done"], s + 1)
                    t = tiles(b * NT + j * 2, 2)
                    nc.gpsimd.tensor_tensor(t, t, m_xn[:, :, :], ALU.add).then_inc(m["res_done"], 1)

                def key_sum(j, b):
                    s = 2 * j + b
                    pool.wait_ge(m["ksq_done"], s + 1)
                    need(pool, m["knorm_done"], s)
                    nc.gpsimd.tensor_tensor(ksum[:, :, :], ksq[:, :, 0:2 * Q], ksq[:, :, 2 * Q:4 * Q], ALU.add).then_inc(m["khalf_done"], 1)
                    pool.wait_ge(m["khalf_done"], s + 1)
                    nc.gpsimd.tensor_tensor(ksum[:, :, 0:Q], ksum[:, :, 0:Q], ksum[:, :, Q:2 * Q], ALU.add).then_inc(m["ksum_done"], 1)

                def sum_up(ops, last_ops, half_done, count, done):
                    for o, a, b, op in ops:
                        last = nc.gpsimd.tensor_tensor(o, a, b, op)
                    last.then_inc(half_done, 1)
                    pool.wait_ge(half_done, count)
                    for o, a, b, op in last_ops:
                        last = nc.gpsimd.tensor_tensor(o, a, b, op)
                    last.then_inc(done, 1)

                def bind_sum(j, b, i):
                    s = 2 * j + b
                    pool.wait_ge(bprod_done[i], s + 1)
                    need(pool, after_done[i], s)
                    p = prod[:, i, :, :]
                    out4 = bound[:, i, :].rearrange("p (c n) -> p c n", n=Q)
                    sum_up([(half_a[:, i, 0:3:2, :], p[:, 0:3:2, :], p[:, 5:8:2, :], ALU.subtract),
                            (half_a[:, i, 1:4:2, :], p[:, 1:4:2, :], p[:, 4:7:2, :], ALU.add),
                            (half_q[:, i, 0:3:2, :], p[:, 10:14:3, :], p[:, 15:7:-7, :], ALU.add),
                            (half_q[:, i, 1:4:2, :], p[:, 11:13:1, :], p[:, 14:8:-5, :], ALU.subtract)],
                           [(out4[:, 0:1, :], half_a[:, i, 0:1, :], half_q[:, i, 0:1, :], ALU.subtract),
                            (out4[:, 1:4, :], half_a[:, i, 1:4, :], half_q[:, i, 1:4, :], ALU.add)],
                           bhalf_done[i], s + 1, bound_done[i])

                def ret_sum(j, b, i):
                    s = 2 * j + b
                    pool.wait_ge(rprod_done[i], s + 1)
                    need(pool, m["normed_done"], s - 1)
                    p = prod[:, i, :, :]
                    out4 = ret[:, b, i, :].rearrange("p (c n) -> p c n", n=Q)
                    sum_up([(half_a[:, i, 0:1, :], p[:, 0:1, :], p[:, 5:6, :], ALU.add),
                            (half_a[:, i, 1:4, :], p[:, 4:13:4, :], p[:, 1:4, :], ALU.subtract),
                            (half_q[:, i, 0:1, :], p[:, 10:11, :], p[:, 15:16, :], ALU.add),
                            (half_q[:, i, 1:4:2, :], p[:, 14:8:-5, :], p[:, 11:5:-5, :], ALU.subtract),
                            (half_q[:, i, 2:3, :], p[:, 7:8, :], p[:, 13:14, :], ALU.subtract)],
                           [(out4, half_a[:, i, :, :], half_q[:, i, :, :], ALU.add)],
                           rhalf_done[i], s + 1, ret_done[i])

                def ret_inverse_std(j, b):
                    s = 2 * j + b
                    pool.wait_ge(m["rstats_done"], s + 1)
                    need(pool, m["normed_done"], s - 1)
                    nc.gpsimd.tensor_tensor(r_var[:, b, :], r_mv[:, b, :, 1], epspos[:, bass.ds(2 * j, 2)], ALU.add).then_inc(m["rvar_done"], 1)
                    pool.wait_ge(m["rvar_done"], 3 * s + 1)
                    nc.gpsimd.tensor_tensor(r_rstd[:, b, :], r_var[:, b, :], minus_half[:, 0:2], ALU.pow).then_inc(m["rvar_done"], 1)
                    pool.wait_ge(m["rvar_done"], 3 * s + 2)
                    nc.gpsimd.tensor_tensor(r_shift[:, b, :], r_mv[:, b, :, 0], r_rstd[:, b, :], ALU.mult).then_inc(m["rvar_done"], 1)
                    pool.wait_ge(m["rvar_done"], 3 * s + 3)
                    nc.gpsimd.tensor_tensor(r_shift[:, b, :], zeros[:, 0:2], r_shift[:, b, :], ALU.subtract).then_inc(m["rrstd_done"], 1)

                pool.wait_ge(consts_ready, 1)
                inverse_std(0, 0)
                inverse_std(0, 1)
                add_normalized(0, 0)
                key_sum(0, 0)

                def body(j, first, last):
                    for b in range(2):
                        nj, nb = (j, 1) if b == 0 else (j + 1, 0)
                        pj, pb = (j, 0) if b == 1 else (j - 1, 1)
                        ahead, behind = not (last and b == 1), not (first and b == 0)
                        bind_sum(j, b, 0)
                        if ahead:
                            add_normalized(nj, nb)
                            key_sum(nj, nb)
                        bind_sum(j, b, 1)
                        if behind:
                            ret_inverse_std(pj, pb)
                        ret_sum(j, b, 0)
                        if not last:
                            inverse_std(j + 1, b)
                        ret_sum(j, b, 1)

                rounds(pool, NP, body)
                ret_inverse_std(NP - 1, 1)
                pool.wait_ge(ffn_sems[0]["xr_done"], NS)
                nc.gpsimd.memset(xnT[:, :, :, 0:1], 0.0).then_inc(shift_zeroed, 1)

            ffn(0)
            mem()
            ffn(1)

        @block.tensor
        def _(pe):
            def prepare():
                pe.wait_ge(lnb_folded, 1)
                for f in range(FC):
                    last = nc.tensor.matmul(o_bank[:, 0, :], lnb_rows[:, f, :], wo[:, f, :], start=f == 0, stop=f == FC - 1)
                last.then_inc(lnb_folded, 1)
                pe.wait_ge(consts_ready, 1)

            prepare()

            def ffn(stage):
                e = ffn_sems[stage]

                def transposes(j, b):
                    s = 2 * j + b
                    pe.wait_ge(e["xn_done"], s + 1)
                    need(pe, e["xnT_done"], s)
                    for f in range(FC):
                        for i in range(CT):
                            last = nc.tensor.transpose(xT_ps[:, f, i * P:(i + 1) * P], xn[:, b, i, f * P:(f + 1) * P], ident[:, :])
                    last.then_inc(e["T_done"], 1)

                def key(j, b):
                    s = 2 * j + b
                    pe.wait_ge(e["xk_done"], s + 1)
                    need(pe, e["relu_done"], s)
                    for o in range(FC):
                        for f in range(FC):
                            last = nc.tensor.matmul(k_ps[:, o, :], wk[:, f, o * P:(o + 1) * P], xk[:, b, f, :],
                                                    start=f == 0, stop=f == FC - 1)
                    last.then_inc(e["k_done"], 1)

                def receptance(j, b):
                    s = 2 * j + b
                    pe.wait_ge(e["xr_done"], s + 1)
                    need(pe, e["gate_done"], s)
                    for i in range(CT):
                        for f in range(FC):
                            last = nc.tensor.matmul(r_tok[:, i, :], xr[:, b, f, i * P:(i + 1) * P], wr[:, f, :],
                                                    start=f == 0, stop=f == FC - 1)
                    last.then_inc(e["r_done"], 1)

                def value(j, b):
                    s = 2 * j + b
                    pe.wait_ge(e["kact_done"], s + 1)
                    need(pe, e["gated_done"], s)
                    for i in range(CT):
                        for f in range(FC):
                            last = nc.tensor.matmul(v_tok[:, i, :], kact[:, f, i * P:(i + 1) * P], wv[:, f, :],
                                                    start=f == 0, stop=f == FC - 1)
                    last.then_inc(e["v_done"], 1)

                if stage == 1:
                    pe.wait_ge(m["x_done"], MS)
                transposes(0, 0)

                def body(j, first, last):
                    for b in range(2):
                        key(j, b)
                        if not (last and b == 1):
                            nj, nb = (j, 1) if b == 0 else (j + 1, 0)
                            transposes(nj, nb)
                        receptance(j, b)
                        value(j, b)

                rounds(pe, NJ, body)

            def mem():
                def transposes(j, b):
                    s = 2 * j + b
                    pe.wait_ge(m["xn_done"], s + 1)
                    need(pe, m["xnT_done"], s)
                    need(pe, m["normedT_done"], s - 2)
                    for f in range(FC):
                        for i in range(2):
                            last = nc.tensor.transpose(t_bank[:, f, i * P:(i + 1) * P], m_xn[:, i, f * P:(f + 1) * P], ident[:, :])
                    last.then_inc(m["T_done"], 1)

                def project(j, b, dst, col, done):
                    for i in range(2):
                        for f in range(FC):
                            nc.tensor.matmul(dst[:, i, :], m_xnT[:, f, i * P:(i + 1) * P], wkv[:, f, col:col + D],
                                             start=f == 0, stop=False)
                        last = nc.tensor.matmul(dst[:, i, :], ones[:, :], bias3[:, col:col + D], start=False, stop=True)
                    last.then_inc(done, 1)

                def keys_values(j, b):
                    s = 2 * j + b
                    pe.wait_ge(m["xnT_done"], s + 1)
                    need(pe, m["khat_done"], s - 1)
                    project(j, b, keys[b], 0, m["K_done"])
                    need(pe, bprod_done[1], s - 1)
                    project(j, b, values[b], D, m["V_done"])

                def sum_upto(j, b, i):
                    s = 2 * j + b
                    pe.wait_ge(bound_done[i], s + 1)
                    nc.tensor.matmul(memory[b], upto[:, :], bound[:, i, :], start=False, stop=True,
                                     skip_group_check=True).then_inc(upto_done[i], 1)

                def sum_after(j, b, i):
                    s = 2 * j + b
                    pe.wait_ge(rprod_done[i], s + 1)
                    nc.tensor.matmul(memory[b], after[:, :], bound[:, i, :], start=False, stop=True,
                                     skip_group_check=True).then_inc(after_done[i], 1)

                def ret_transposes(j, b):
                    s = 2 * j + b
                    pe.wait_ge(m["normed_done"], s + 1)
                    ahead = s + 3 if not isinstance(s, int) else min(s + 3, MS)
                    pe.wait_ge(m["xnT_done"], ahead)
                    for f in range(FC):
                        for i in range(2):
                            last = nc.tensor.transpose(t_bank[:, f, i * P:(i + 1) * P], normed[:, i, f * P:(f + 1) * P], ident[:, :])
                    last.then_inc(m["nT_done"], 1)

                def output(j, b):
                    s = 2 * j + b
                    pe.wait_ge(m["normedT_done"], s + 1)
                    need(pe, m["x_done"], s)
                    for i in range(2):
                        for f in range(FC):
                            nc.tensor.matmul(o_bank[:, i, :], normedT[:, f, i * P:(i + 1) * P], wo[:, f, :],
                                             start=f == 0, stop=False)
                        last = nc.tensor.matmul(o_bank[:, i, :], ones[:, :], bias3[:, 2 * D:], start=False, stop=True)
                    last.then_inc(m["O_done"], 1)

                pe.wait_ge(ffn_sems[0]["gated_done"], NS)
                for b in range(2):
                    nc.tensor.matmul(memory[b], upto[:, :], zeros[:, :], start=True, stop=True, skip_group_check=True)
                transposes(0, 0)
                keys_values(0, 0)

                def body(j, first, last):
                    for b in range(2):
                        nj, nb = (j, 1) if b == 0 else (j + 1, 0)
                        pj, pb = (j, 0) if b == 1 else (j - 1, 1)
                        ahead, behind = not (last and b == 1), not (first and b == 0)
                        if ahead:
                            transposes(nj, nb)
                            keys_values(nj, nb)
                        sum_upto(j, b, 0)
                        sum_after(j, b, 0)
                        sum_upto(j, b, 1)
                        if behind:
                            ret_transposes(pj, pb)
                            output(pj, pb)
                        sum_after(j, b, 1)

                rounds(pe, NP, body)
                ret_transposes(NP - 1, 1)
                output(NP - 1, 1)

            ffn(0)
            mem()
            ffn(1)


CONST_LOADS = 8
POOL_CONSTS = 2


def kernel(L0_attn_x, L0_attn_Wk, L0_attn_bk, L0_attn_Wv, L0_attn_bv, L0_attn_ln_g, L0_attn_ln_b, L0_attn_Wo, L0_attn_bo,
           L0_ffn_W_r, L0_ffn_W_k, L0_ffn_W_v, L0_ffn_mu_r, L0_ffn_mu_k):
    import numpy as np
    import concourse.bacc as bacc
    from concourse.bass_utils import run_bass_kernel_spmd

    def by_component(a):
        a = np.asarray(a)
        return a.reshape(a.shape[0] // 4, 4, -1).transpose(1, 0, 2).reshape(a.shape)

    arrays = {
        "x": np.asarray(L0_attn_x),
        "w_kv": np.concatenate([by_component(L0_attn_Wk).T, by_component(L0_attn_Wv).T], axis=1),
        "w_o": by_component(np.asarray(L0_attn_Wo).T),
        "w_r": np.asarray(L0_ffn_W_r).T,
        "w_k": np.asarray(L0_ffn_W_k).T,
        "w_v": np.asarray(L0_ffn_W_v).T,
        "b_kv": np.concatenate([by_component(L0_attn_bk), by_component(L0_attn_bv)]),
        "b_o": np.asarray(L0_attn_bo),
        "columns": np.concatenate([v.reshape(-1, P).T for v in (np.asarray(L0_ffn_mu_r), np.asarray(L0_ffn_mu_k),
                                                                by_component(L0_attn_ln_g), by_component(L0_attn_ln_b))], axis=1),
    }
    arrays = {name: np.ascontiguousarray(a) for name, a in arrays.items()}
    nc = bacc.Bacc("TRN2", target_bir_lowering=False, num_devices=1)
    args = [nc.dram_tensor(name, a.shape, mybir.dt.from_np(a.dtype), kind="ExternalInput").ap() for name, a in arrays.items()]
    out = nc.dram_tensor("out", arrays["x"].shape, F32, kind="ExternalOutput").ap()
    macaron(nc, *args, out)
    r = run_bass_kernel_spmd(nc, [arrays], core_ids=[0])
    return r.results[0]["out"]
```

```python
from contextlib import ExitStack

import concourse.bass as bass
from concourse import mybir

F32 = mybir.dt.float32
F32R = mybir.dt.float32r
BF16 = mybir.dt.bfloat16
I32 = mybir.dt.int32
ALU = mybir.AluOpType
ACT = mybir.ActivationFunctionType

P = 128
LN_EPS = 1e-5
NORM_EPS = 1e-12
STAT = 6


def need(engine, semaphore, count):
    if isinstance(count, int) and count <= 0:
        return
    engine.wait_ge(semaphore, count)


def rounds(engine, n, body):
    body(0, True, False)
    with engine.Fori(1, n - 1) as j:
        body(j, False, False)
    body(n - 1, False, True)


def macaron(nc, x, w_kv, w_o, w_r, w_k, w_v, b_kv, b_o, columns, out):
    B, L, D = x.shape
    FC = D // P
    NT = L // P
    Q = D // 4
    CT = 4
    CW = CT * P
    NJ = NT // CT
    NP = NT // 2
    NS = B * NJ
    MS = B * NP
    assert B == 2 and D == 2 * P and L % CW == 0

    with ExitStack() as ctx:
        def sb(name, shape, dt=F32):
            return ctx.enter_context(nc.sbuf_tensor(name, shape, dt))

        def sem(name):
            return ctx.enter_context(nc.semaphore(name))

        res = sb("res", [P, B * NT * D])
        wkv = sb("wkv", [P, FC, 2 * D])
        wo = sb("wo", [P, FC, D])
        wffn = sb("wffn", [P, 3, FC, D])
        wffn_hi = sb("wffn_hi", [P, 3, FC, D], F32R)
        wffn_lo = sb("wffn_lo", [P, 3, FC, D], F32R)
        cols = sb("cols", [P, 4 * FC])
        mur, muk, lng, lnb = (cols[:, i * FC:(i + 1) * FC] for i in range(4))
        lnb_rows = sb("lnb_rows", [P, FC, P])
        bias = sb("bias", [P, 3 * D])
        bias_rest = sb("bias_rest", [P, 3 * D])
        bias_mid = sb("bias_mid", [P, 3 * D], BF16)
        bias_part = sb("bias_part", [P, 3 * D], BF16)
        bias3 = sb("bias3", [P, 3 * D], BF16)
        ones = sb("ones", [P, P], BF16)
        ident = sb("ident", [P, P])
        upto = sb("upto", [P, P])
        after = sb("after", [P, P])
        zeros = sb("zeros", [P, D])
        pos = sb("pos", [P, NT], I32)
        eps4 = sb("eps4", [P, NP, 4])
        minus_half = sb("minus_half", [P, CT])
        eps_tile = sb("eps_tile", [P, CT])
        spare = sb("spare", [P, 1])

        st = sb("st", [P, 2, CT, STAT])
        mv = sb("mv", [P, 2, CT, 2])
        rstd = sb("rstd", [P, 2, CT])
        xn = sb("xn", [P, 2, CT, D])
        xnT = sb("xnT", [P, 2, FC, CW + 1])
        diff = sb("diff", [P, FC, CW])
        xk = sb("xk", [P, FC, CW])
        xk_hi = sb("xk_hi", [P, FC, CW], F32R)
        xk_lo = sb("xk_lo", [P, FC, CW], F32R)
        xr = sb("xr", [P, FC, CW])
        xr_hi = sb("xr_hi", [P, FC, CW], F32R)
        xr_lo = sb("xr_lo", [P, FC, CW], F32R)
        relu_k = sb("relu_k", [P, FC, CW])
        kact = sb("kact", [P, FC, CW])
        kact_hi = sb("kact_hi", [P, FC, CW], F32R)
        kact_lo = sb("kact_lo", [P, FC, CW], F32R)
        gating_buffers = sb("gating_buffers", [P, 2, CT * D])
        gate, gated = (gating_buffers[:, i, :].rearrange("p (t n) -> p t n", n=D) for i in range(2))

        n_st = sb("n_st", [P, 2, 4, STAT])
        n_mv = sb("n_mv", [P, 2, 4, 2])
        n_var = sb("n_var", [P, 2, 4])
        n_std = sb("n_std", [P, 2, 4])
        n_rstd = sb("n_rstd", [P, 2, 4])
        n_shift = sb("n_shift", [P, 2, 4])
        n_gain = sb("n_gain", [P, 2, 2])
        m_xn = sb("m_xn", [P, 2, D])
        m_xnT = sb("m_xnT", [P, FC, 2 * P])
        ksq = sb("ksq", [P, 2, D])
        ksum = sb("ksum", [P, 2, 2 * Q])
        knorm = sb("knorm", [P, 2, Q])
        kinv = sb("kinv", [P, 2, Q])
        khat = sb("khat", [P, 2, 2, D])
        bprod = xn[:, :, :, :].rearrange("p i t (c n) -> p i (t c) n", n=Q)
        rprod = gating_buffers[:, :, :].rearrange("p i (c n) -> p i c n", n=Q)
        bhalf = sb("bhalf", [P, 2, 2, 4, Q])
        rhalf = sb("rhalf", [P, 2, 2, 4, Q])
        bound = sb("bound", [P, 2, D])
        ret = sb("ret", [P, 2, 2, D])
        normed = sb("normed", [P, 2, D])
        normedT = sb("normedT", [P, FC, 2 * P])

        bank = [ctx.enter_context(nc.psum_tensor(f"bank{i}", [P, 2, 512], F32)) for i in range(4)]
        xT_ps, k_ps, r_ps, v_ps = (t[:, :, :] for t in bank)
        r_tok = r_ps.rearrange("p h (t n) -> p (h t) n", n=D)
        v_tok = v_ps.rearrange("p h (t n) -> p (h t) n", n=D)
        t_bank = bank[0][:, 0, :].rearrange("p (f t) -> p f t", f=FC)
        o_bank = bank[0][:, 1, :].rearrange("p (t n) -> p t n", t=2)
        keys = [bank[1][:, b, :].rearrange("p (t n) -> p t n", t=2) for b in range(2)]
        values = [bank[2][:, b, :].rearrange("p (t n) -> p t n", t=2) for b in range(2)]
        memory = [bank[3][:, b, 0:D] for b in range(2)]

        def tiles(tile, n):
            return res[:, bass.ds(tile * D, n * D)].rearrange("p (t n) -> p t n", n=D)

        def rows(dram, b, j, n):
            return dram[b, bass.ds(j * (n * P), n * P), :].rearrange("(t p) n -> p t n", p=P)

        consts_in = sem("consts_in")
        late_consts_in = sem("late_consts_in")
        consts_pool = sem("consts_pool")
        setup = sem("setup")
        lnb_folded = sem("lnb_folded")
        weights_ready = sem("weights_ready")
        mem_ready = sem("mem_ready")
        shift_zeroed = sem("shift_zeroed")
        x_in = [sem(f"x_in{b}") for b in range(2)]
        x_out = [sem(f"x_out{b}") for b in range(2)]

        FFN_SEMS = ["st_done", "stats_done", "var_done", "rstd_done", "xn_done", "T_done", "carry_done", "xnT_done",
                    "diff_done", "xk_done", "xkhi_done", "xklo_done", "xr_done", "xrhi_done", "xrlo_done", "k_done",
                    "relu_done", "kact_done", "kacthi_done", "kactlo_done", "r_done", "gate_done", "v_done", "gated_done",
                    "res_done"]
        ffn_sems = [{n: sem(f"f{i}_{n}") for n in FFN_SEMS} for i in range(2)]
        MEM_SEMS = ["st_done", "mv_done", "var_done", "std_done", "rstd_done", "scales_done", "xn_done", "T_done", "xnT_done",
                    "res_done", "K_done", "V_done", "ksq_done", "khalf_done", "ksum_done", "knorm_done", "kmax_done",
                    "kinv_done", "khat_done", "normed_done", "nT_done", "normedT_done", "O_done", "x_done"]
        m = {n: sem(f"m_{n}") for n in MEM_SEMS}

        def for_tiles(name):
            return [sem(f"m_{name}{i}_done") for i in range(2)]

        bprod_done, bhalf_done, bound_done = for_tiles("bprod"), for_tiles("bhalf"), for_tiles("bound")
        rprod_done, rhalf_done, ret_done = for_tiles("rprod"), for_tiles("rhalf"), for_tiles("ret")
        upto_done, after_done = for_tiles("upto"), for_tiles("after")

        def x_ready(engine, stage, b, j):
            if stage == 0:
                engine.wait_ge(x_in[b], 16 * (j + 1))
            else:
                engine.wait_ge(m["x_done"], MS)

        block = ctx.enter_context(nc.Block())

        def sum_up(engine, first, then, half_done, count, done):
            for o, a, b, op in first:
                last = engine.tensor_tensor(o, a, b, op)
            last.then_inc(half_done, 1)
            engine.wait_ge(half_done, count)
            for o, a, b, op in then:
                last = engine.tensor_tensor(o, a, b, op)
            last.then_inc(done, 1)

        def bind_sum(engine, j, b, i):
            s = 2 * j + b
            engine.wait_ge(bprod_done[i], s + 1)
            need(engine, after_done[i], s)
            p, ha, hq = bprod[:, i, :, :], bhalf[:, i, 0, :, :], bhalf[:, i, 1, :, :]
            out4 = bound[:, i, :].rearrange("p (c n) -> p c n", n=Q)
            sum_up(engine,
                   [(ha[:, 0:3:2, :], p[:, 0:3:2, :], p[:, 5:8:2, :], ALU.subtract),
                    (ha[:, 1:4:2, :], p[:, 1:4:2, :], p[:, 4:7:2, :], ALU.add),
                    (hq[:, 0:3:2, :], p[:, 10:14:3, :], p[:, 15:7:-7, :], ALU.add),
                    (hq[:, 1:4:2, :], p[:, 11:13:1, :], p[:, 14:8:-5, :], ALU.subtract)],
                   [(out4[:, 0:1, :], ha[:, 0:1, :], hq[:, 0:1, :], ALU.subtract),
                    (out4[:, 1:4, :], ha[:, 1:4, :], hq[:, 1:4, :], ALU.add)],
                   bhalf_done[i], s + 1, bound_done[i])

        def ret_sum(engine, j, b, i):
            s = 2 * j + b
            engine.wait_ge(rprod_done[i], s + 1)
            need(engine, m["normed_done"], s - 1)
            p, ha, hq = rprod[:, i, :, :], rhalf[:, i, 0, :, :], rhalf[:, i, 1, :, :]
            out4 = ret[:, b, i, :].rearrange("p (c n) -> p c n", n=Q)
            sum_up(engine,
                   [(ha[:, 0:1, :], p[:, 0:1, :], p[:, 5:6, :], ALU.add),
                    (ha[:, 1:4, :], p[:, 4:13:4, :], p[:, 1:4, :], ALU.subtract),
                    (hq[:, 0:1, :], p[:, 10:11, :], p[:, 15:16, :], ALU.add),
                    (hq[:, 1:4:2, :], p[:, 14:8:-5, :], p[:, 11:5:-5, :], ALU.subtract),
                    (hq[:, 2:3, :], p[:, 7:8, :], p[:, 13:14, :], ALU.subtract)],
                   [(out4, ha, hq, ALU.add)],
                   rhalf_done[i], s + 1, ret_done[i])

        @block.sync
        def _(sp):
            def load_x(b, j):
                sp.dma_start(tiles(b * NT + j * CT, CT), rows(x, b, j, CT)).then_inc(x_in[b], 16)

            load_x(0, 0)
            for i, w in enumerate((w_k, w_r, w_v)):
                sp.dma_start(wffn[:, i, :, :], w.rearrange("(f p) n -> p f n", p=P)).then_inc(consts_in, 16)
            sp.dma_start(cols[:, :], columns).then_inc(consts_in, 16)
            load_x(1, 0)
            for dst, src in ((wkv[:, :, :], w_kv.rearrange("(f p) n -> p f n", p=P)),
                             (wo[:, :, :], w_o.rearrange("(f p) n -> p f n", p=P)),
                             (bias[:, 0:2 * D], b_kv.partition_broadcast(P)),
                             (bias[:, 2 * D:], b_o.partition_broadcast(P))):
                sp.dma_start(dst, src).then_inc(late_consts_in, 16)
            with sp.Fori(1, NJ) as j:
                for b in range(2):
                    sp.wait_ge(x_in[b], 16 * j)
                    load_x(b, j)
            done = ffn_sems[1]["res_done"]
            with sp.Fori(0, NJ) as j:
                for b in range(2):
                    sp.wait_ge(done, 2 * j + b + 1)
                    sp.dma_start(rows(out, b, j, CT), tiles(b * NT + j * CT, CT)).then_inc(x_out[b], 16)
            for b in range(2):
                sp.wait_ge(x_out[b], 16 * NJ)

        @block.vector
        def _(dve):
            own_steps = 0

            def own(instruction):
                nonlocal own_steps
                own_steps += 1
                instruction.then_inc(setup, 1)
                dve.wait_ge(setup, own_steps)

            def prepare_ffn():
                dve.wait_ge(consts_in, 16 * 4)
                own(nc.vector.tensor_scalar(wffn[:, 2, :, :], wffn[:, 2, :, :], 0.5, None, ALU.mult))
                own(nc.vector.tensor_copy(wffn_hi[:, :, :, :], wffn[:, :, :, :]))
                nc.vector.tensor_tensor(wffn_lo[:, :, :, :], wffn[:, :, :, :], wffn_hi[:, :, :, :].bitcast(F32),
                                        ALU.subtract).then_inc(weights_ready, 1)

            def prepare_memory():
                dve.wait_ge(late_consts_in, 16 * 4)
                own(nc.vector.tensor_copy(lnb_rows[:, :, :], lnb.unsqueeze(2).to_broadcast([P, FC, P])))
                own(nc.vector.memset(bias3[:, :], 0.0))
                nc.vector.memset(ones[:, :], 1.0).then_inc(lnb_folded, 1)
                dve.wait_ge(lnb_folded, 2)
                own(nc.vector.tensor_tensor(bias[:, 2 * D:], v_tok[:, 0, :], bias[:, 2 * D:], ALU.add))
                for f in range(FC):
                    nc.vector.tensor_scalar(wo[:, f, :], wo[:, f, :], lng[:, f:f + 1], None, ALU.mult)
                own(nc.vector.tensor_copy(bias_part[:, :], bias[:, :]))
                nc.vector.tensor_copy(bias3[0:1, :], bias_part[0:1, :])
                own(nc.vector.tensor_tensor(bias_rest[:, :], bias[:, :], bias_part[:, :], ALU.subtract))
                own(nc.vector.tensor_copy(bias_mid[:, :], bias_rest[:, :]))
                nc.vector.tensor_copy(bias3[32:33, :], bias_mid[32:33, :])
                own(nc.vector.tensor_tensor(bias_rest[:, :], bias_rest[:, :], bias_mid[:, :], ALU.subtract))
                own(nc.vector.tensor_copy(bias3[64:65, :], bias_rest[64:65, :]))
                nc.vector.tensor_scalar(eps4[:, :, 0:2], pos[:, :].rearrange("p (j i) -> p j i", i=2), LN_EPS, None, ALU.mult)
                nc.vector.memset(eps4[:, :, 2:4], LN_EPS).then_inc(mem_ready, 1)

            def ffn(stage):
                e = ffn_sems[stage]

                def stats(j, b):
                    x_ready(dve, stage, b, j)
                    t = tiles(b * NT + j * CT, CT)
                    for i in range(CT):
                        last = nc.vector.bn_stats(st[:, b, i, :], t[:, i, :])
                    last.then_inc(e["st_done"], 1)

                def aggregate(j, b):
                    for i in range(CT):
                        last = nc.vector.bn_aggr(mv[:, b, i, :], st[:, b, i, :])
                    last.then_inc(e["stats_done"], 1)

                def normalize(j, b):
                    s = 2 * j + b
                    dve.wait_ge(e["rstd_done"], s + 1)
                    need(dve, e["T_done"], s - 1)
                    t = tiles(b * NT + j * CT, CT)
                    for i in range(CT):
                        last = nc.vector.tensor_scalar(xn[:, b, i, :], t[:, i, :], mv[:, b, i, 0:1], rstd[:, b, i:i + 1],
                                                       ALU.subtract, ALU.mult)
                    last.then_inc(e["xn_done"], 1)

                def difference(j, b):
                    s = 2 * j + b
                    dve.wait_ge(e["xnT_done"], s + 1)
                    need(dve, e["xr_done"], s)
                    nc.vector.tensor_tensor(diff[:, :, :], xnT[:, b, :, 1:CW + 1], xnT[:, b, :, 0:CW],
                                            ALU.subtract).then_inc(e["diff_done"], 1)

                def mix(j, b, dst, mu, read, done):
                    s = 2 * j + b
                    dve.wait_ge(e["diff_done"], s + 1)
                    for semaphore in read:
                        need(dve, e[semaphore], s)
                    for f in range(FC):
                        last = nc.vector.scalar_tensor_tensor(dst[:, f, :], diff[:, f, :], mu[:, f:f + 1],
                                                              xnT[:, b, f, 0:CW], ALU.mult, ALU.add)
                    last.then_inc(e[done], 1)

                def square_low(j, b, o):
                    s = 2 * j + b
                    dve.wait_ge(e["kacthi_done"], 2 * s + o + 1)
                    nc.vector.tensor_tensor(kact_lo[:, o, :], kact[:, o, :], kact_hi[:, o, :].bitcast(F32),
                                            ALU.subtract).then_inc(e["kactlo_done"], 1)

                def gating(j, b):
                    s = 2 * j + b
                    dve.wait_ge(e["gate_done"], s + 1)
                    dve.wait_ge(e["v_done"], s + 1)
                    need(dve, e["res_done"], s)
                    nc.vector.tensor_tensor(gated, v_tok, gate, ALU.mult).then_inc(e["gated_done"], 1)

                def mix_key(j, b):
                    mix(j, b, xk, muk, ["xkhi_done", "xklo_done"], "xk_done")

                def mix_receptance(j, b):
                    mix(j, b, xr, mur, ["xrhi_done", "xrlo_done"], "xr_done")

                def own_wait(s):
                    dve.wait_ge(e["st_done"], s + 1)
                    nc.vector.memset(spare[:, :], 0.0)

                for b in range(2):
                    stats(0, b)
                    own_wait(b)
                    aggregate(0, b)
                    normalize(0, b)
                    if stage == 0 and b == 0:
                        prepare_ffn()
                difference(0, 0)
                mix_key(0, 0)
                mix_receptance(0, 0)
                if stage == 0:
                    prepare_memory()

                def body(j, first, last):
                    for b in range(2):
                        nj, nb = (j, 1) if b == 0 else (j + 1, 0)
                        ahead = not (last and b == 1)
                        if not (first and b == 0):
                            gating(*((j, 0) if b == 1 else (j - 1, 1)))
                        if not last:
                            stats(j + 1, b)
                        if ahead:
                            difference(nj, nb)
                        square_low(j, b, 0)
                        if not last:
                            own_wait(2 * j + b + 2)
                            aggregate(j + 1, b)
                        if ahead:
                            mix_key(nj, nb)
                        square_low(j, b, 1)
                        if ahead:
                            mix_receptance(nj, nb)
                        if not last:
                            normalize(j + 1, b)

                rounds(dve, NJ, body)
                gating(NJ - 1, 1)

            def mem():
                def ln_stats(r, ret_at, res_at):
                    q, n = r
                    need(dve, m["res_done"], n - 1 if not isinstance(n, int) else min(n - 1, MS))
                    need(dve, m["normed_done"], n - 4)
                    if ret_at is not None:
                        pj, pb = ret_at
                        for i in range(2):
                            dve.wait_ge(ret_done[i], n - 2)
                            last = nc.vector.bn_stats(n_st[:, q, i, :], ret[:, pb, i, :])
                    if res_at is not None:
                        jj, bb = res_at
                        t = tiles(bb * NT + jj * 2, 2)
                        for i in range(2):
                            last = nc.vector.bn_stats(n_st[:, q, 2 + i, :], t[:, i, :])
                    last.then_inc(m["st_done"], 1)

                def ln_variance(r, ret_at, res_at):
                    q, n = r
                    lo, hi = (0 if ret_at is not None else 2), (4 if res_at is not None else 2)
                    for i in range(lo, hi):
                        last = nc.vector.bn_aggr(n_mv[:, q, i, :], n_st[:, q, i, :])
                    last.then_inc(m["mv_done"], 1)
                    dve.wait_ge(m["mv_done"], n + 1)
                    pj = ret_at[0] if ret_at is not None else 0
                    nc.vector.tensor_tensor(n_var[:, q, lo:hi], n_mv[:, q, lo:hi, 1],
                                            eps4[:, bass.ds(pj, 1), lo:hi].rearrange("p j i -> p (j i)"), ALU.add).then_inc(m["var_done"], 1)

                def ln_scales(r, ret_at, res_at):
                    q, n = r
                    lo, hi = (0 if ret_at is not None else 2), (4 if res_at is not None else 2)
                    dve.wait_ge(m["std_done"], n + 1)
                    nc.vector.reciprocal(n_rstd[:, q, lo:hi], n_std[:, q, lo:hi]).then_inc(m["rstd_done"], 1)
                    dve.wait_ge(m["rstd_done"], n + 1)
                    if res_at is not None:
                        nc.vector.tensor_scalar(n_gain[:, q, :], n_rstd[:, q, 2:4], 1.0, None, ALU.add)
                    nc.vector.scalar_tensor_tensor(n_shift[:, q, lo:hi], n_mv[:, q, lo:hi, 0], -1.0, n_rstd[:, q, lo:hi],
                                                   ALU.mult, ALU.mult).then_inc(m["scales_done"], 1)

                def key_inverse(j, b):
                    s = 2 * j + b
                    dve.wait_ge(m["knorm_done"], s + 1)
                    need(dve, m["khat_done"], s)
                    nc.vector.tensor_scalar(knorm[:, :, :], knorm[:, :, :], NORM_EPS, None, ALU.max).then_inc(m["kmax_done"], 1)
                    dve.wait_ge(m["kmax_done"], s + 1)
                    nc.vector.reciprocal(kinv[:, :, :], knorm[:, :, :]).then_inc(m["kinv_done"], 1)

                def key_unit(j, b):
                    s = 2 * j + b
                    dve.wait_ge(m["kinv_done"], s + 1)
                    dve.wait_ge(m["ksq_done"], s + 1)
                    need(dve, rprod_done[1], s - 1)
                    nc.vector.tensor_tensor(khat[:, b, :, :].rearrange("p t (c n) -> p t c n", n=Q),
                                            keys[b].rearrange("p t (c n) -> p t c n", n=Q),
                                            kinv[:, :, :].unsqueeze(2).to_broadcast([P, 2, 4, Q]), ALU.mult).then_inc(m["khat_done"], 1)

                def all_products(dst, b, i, of, done):
                    nc.vector.tensor_tensor(
                        dst[:, i, :, :].rearrange("p (a b) n -> p a b n", a=4),
                        of.rearrange("p (a n) -> p a n", n=Q).unsqueeze(2).to_broadcast([P, 4, 4, Q]),
                        khat[:, b, i, :].rearrange("p (b n) -> p b n", n=Q).unsqueeze(1).to_broadcast([P, 4, 4, Q]),
                        ALU.mult).then_inc(done, 1)

                def bind(j, b, i):
                    s = 2 * j + b
                    dve.wait_ge(m["khat_done"], s + 1)
                    dve.wait_ge(m["V_done"], s + 1)
                    need(dve, bound_done[i], s)
                    all_products(bprod, b, i, values[b][:, i, :], bprod_done[i])

                def retrieve(j, b, i):
                    s = 2 * j + b
                    need(dve, ret_done[i], s)
                    dve.wait_ge(upto_done[i], s + 1)
                    all_products(rprod, b, i, memory[b], rprod_done[i])

                def residual(j, b):
                    s = 2 * j + b
                    dve.wait_ge(m["O_done"], s + 1)
                    dve.wait_ge(m["res_done"], s + 1)
                    t = tiles(b * NT + j * 2, 2)
                    nc.vector.tensor_tensor(t, o_bank, t, ALU.add).then_inc(m["x_done"], 1)

                dve.wait_ge(ffn_sems[0]["res_done"], NS)
                for b in range(2):
                    r = (b, b)
                    ln_stats(r, None, (0, b))
                    dve.wait_ge(m["st_done"], b + 1)
                    ln_variance(r, None, (0, b))
                    ln_scales(r, None, (0, b))
                key_inverse(0, 0)
                key_unit(0, 0)
                bind(0, 0, 0)
                bind(0, 0, 1)

                def body(j, first, last):
                    for b in range(2):
                        s = 2 * j + b
                        nj, nb = (j, 1) if b == 0 else (j + 1, 0)
                        pj, pb = (j, 0) if b == 1 else (j - 1, 1)
                        ahead, behind = not (last and b == 1), not (first and b == 0)
                        r = (b, s + 2)
                        parts = (pj, pb) if behind else None, (j + 1, b) if not last else None
                        some = behind or not last
                        if some:
                            ln_stats(r, *parts)
                            dve.wait_ge(m["st_done"], s + 3)
                        retrieve(j, b, 0)
                        if some:
                            ln_variance(r, *parts)
                        ret_sum(nc.vector, j, b, 0)
                        if some:
                            ln_scales(r, *parts)
                        retrieve(j, b, 1)
                        if ahead:
                            key_inverse(nj, nb)
                            key_unit(nj, nb)
                            bind(nj, nb, 0)
                            bind(nj, nb, 1)
                        if behind:
                            residual(pj, pb)

                rounds(dve, NP, body)
                r, at = (0, MS + 2), (NP - 1, 1)
                ln_stats(r, at, None)
                dve.wait_ge(m["st_done"], MS + 3)
                ln_variance(r, at, None)
                ln_scales(r, at, None)
                residual(*at)

            ffn(0)
            mem()
            ffn(1)

        @block.scalar
        def _(act):
            def ffn(stage):
                e = ffn_sems[stage]

                def evict_xT(j, b, first):
                    s = 2 * j + b
                    act.wait_ge(e["T_done"], s + 1)
                    need(act, e["xr_done"], s - 1)
                    if not first:
                        nc.scalar.copy(xnT[:, b, :, 0:1], xnT[:, b, :, CW:CW + 1]).then_inc(e["carry_done"], 1)
                        act.wait_ge(e["carry_done"], s - 1)
                    nc.scalar.copy(xnT[:, b, :, 1:CW + 1], xT_ps).then_inc(e["xnT_done"], 1)

                def key_high(j, b):
                    s = 2 * j + b
                    act.wait_ge(e["xk_done"], s + 1)
                    need(act, e["k_done"], 2 * s)
                    nc.scalar.copy(xk_hi[:, :, :], xk[:, :, :]).then_inc(e["xkhi_done"], 1)

                def receptance_high(j, b):
                    s = 2 * j + b
                    act.wait_ge(e["xr_done"], s + 1)
                    need(act, e["r_done"], s)
                    nc.scalar.copy(xr_hi[:, :, :], xr[:, :, :]).then_inc(e["xrhi_done"], 1)

                def key_activation(j, b, o):
                    s = 2 * j + b
                    act.wait_ge(e["k_done"], 2 * s + o + 1)
                    need(act, e["kactlo_done"], 2 * s)
                    nc.scalar.activation(relu_k[:, o, :], k_ps[:, o, :], ACT.Relu).then_inc(e["relu_done"], 1)
                    act.wait_ge(e["relu_done"], 2 * s + o + 1)
                    nc.scalar.activation(kact[:, o, :], relu_k[:, o, :], ACT.Square).then_inc(e["kact_done"], 1)
                    act.wait_ge(e["kact_done"], 2 * s + o + 1)
                    need(act, e["v_done"], s)
                    nc.scalar.copy(kact_hi[:, o, :], kact[:, o, :]).then_inc(e["kacthi_done"], 1)

                def sigmoid(j, b):
                    s = 2 * j + b
                    act.wait_ge(e["r_done"], s + 1)
                    need(act, e["gated_done"], s)
                    nc.scalar.activation(gate, r_tok, ACT.Sigmoid).then_inc(e["gate_done"], 1)

                if stage == 0:
                    act.wait_ge(consts_pool, POOL_CONSTS)
                else:
                    act.wait_ge(shift_zeroed, 1)
                evict_xT(0, 0, True)
                key_high(0, 0)
                receptance_high(0, 0)

                def body(j, first, last):
                    for b in range(2):
                        nj, nb = (j, 1) if b == 0 else (j + 1, 0)
                        ahead = not (last and b == 1)
                        if ahead:
                            evict_xT(nj, nb, first and b == 0)
                        key_activation(j, b, 0)
                        key_activation(j, b, 1)
                        if ahead:
                            key_high(nj, nb)
                        sigmoid(j, b)
                        if ahead:
                            receptance_high(nj, nb)

                rounds(act, NJ, body)

            def mem():
                def std(r, lo, hi):
                    q, n = r
                    act.wait_ge(m["var_done"], n + 1)
                    nc.scalar.activation(n_std[:, q, lo:hi], n_var[:, q, lo:hi], ACT.Sqrt).then_inc(m["std_done"], 1)

                def normalize(j, b):
                    s = 2 * j + b
                    act.wait_ge(m["scales_done"], s + 1)
                    need(act, m["T_done"], s)
                    t = tiles(b * NT + j * 2, 2)
                    for i in range(2):
                        last = nc.scalar.activation(m_xn[:, i, :], t[:, i, :], ACT.Identity, bias=n_shift[:, b, 2 + i:3 + i],
                                                    scale=n_rstd[:, b, 2 + i:3 + i])
                    last.then_inc(m["xn_done"], 1)

                def add_normalized(j, b):
                    t = tiles(b * NT + j * 2, 2)
                    for i in range(2):
                        last = nc.scalar.activation(t[:, i, :], t[:, i, :], ACT.Identity, bias=n_shift[:, b, 2 + i:3 + i],
                                                    scale=n_gain[:, b, i:i + 1])
                    last.then_inc(m["res_done"], 1)

                def evict_xT(j, b):
                    s = 2 * j + b
                    act.wait_ge(m["T_done"], s + 1)
                    need(act, m["V_done"], s)
                    nc.scalar.copy(m_xnT[:, :, :], t_bank).then_inc(m["xnT_done"], 1)

                def key_square(j, b):
                    s = 2 * j + b
                    act.wait_ge(m["K_done"], s + 1)
                    need(act, m["ksum_done"], s)
                    nc.scalar.activation(ksq[:, :, :], keys[b], ACT.Square).then_inc(m["ksq_done"], 1)

                def key_norm(j, b):
                    s = 2 * j + b
                    act.wait_ge(m["ksum_done"], s + 1)
                    need(act, m["kinv_done"], s)
                    nc.scalar.activation(knorm[:, :, :], ksum[:, :, 0:Q], ACT.Sqrt).then_inc(m["knorm_done"], 1)

                def ret_normalize(j, b):
                    s = 2 * j + b
                    act.wait_ge(m["scales_done"], s + 4)
                    need(act, m["nT_done"], s)
                    q = 1 - b
                    for i in range(2):
                        last = nc.scalar.activation(normed[:, i, :], ret[:, b, i, :], ACT.Identity, bias=n_shift[:, q, i:i + 1],
                                                    scale=n_rstd[:, q, i:i + 1])
                    last.then_inc(m["normed_done"], 1)

                def evict_nT(j, b):
                    s = 2 * j + b
                    act.wait_ge(m["nT_done"], s + 1)
                    need(act, m["O_done"], s)
                    nc.scalar.copy(normedT[:, :, :], t_bank).then_inc(m["normedT_done"], 1)

                std((0, 0), 2, 4)
                normalize(0, 0)
                evict_xT(0, 0)
                add_normalized(0, 0)
                std((1, 1), 2, 4)
                normalize(0, 1)
                key_square(0, 0)
                evict_xT(0, 1)
                key_norm(0, 0)
                add_normalized(0, 1)

                def body(j, first, last):
                    for b in range(2):
                        nj, nb = (j, 1) if b == 0 else (j + 1, 0)
                        pj, pb = (j, 0) if b == 1 else (j - 1, 1)
                        ahead, behind = not (last and b == 1), not (first and b == 0)
                        if behind or not last:
                            std((b, 2 * j + b + 2), 0 if behind else 2, 2 if last else 4)
                        if ahead:
                            key_square(nj, nb)
                        if behind:
                            ret_normalize(pj, pb)
                        if ahead:
                            key_norm(nj, nb)
                        if not last:
                            normalize(j + 1, b)
                        if behind:
                            evict_nT(pj, pb)
                        if not last:
                            evict_xT(j + 1, b)
                            add_normalized(j + 1, b)

                rounds(act, NP, body)
                std((0, MS + 2), 0, 2)
                ret_normalize(NP - 1, 1)
                evict_nT(NP - 1, 1)

            ffn(0)
            mem()
            ffn(1)

        @block.gpsimd
        def _(pool):
            def prepare():
                nc.gpsimd.memset(ident[:, :], 0.0)
                nc.gpsimd.memset(upto[:, :], 1.0)
                nc.gpsimd.memset(after[:, :], 1.0)
                nc.gpsimd.memset(zeros[:, :], 0.0)
                nc.gpsimd.memset(xnT[:, :, :, 0:1], 0.0)
                nc.gpsimd.memset(minus_half[:, :], -0.5)
                nc.gpsimd.memset(eps_tile[:, :], LN_EPS)
                nc.gpsimd.iota(pos[:, :], pattern=[[P, NT]], base=1, channel_multiplier=1).then_inc(consts_pool, 1)
                pool.wait_ge(consts_pool, 1)
                nc.gpsimd.affine_select(out=ident[:, :], in_=ident[:, :], compare_op=ALU.not_equal, fill=1.0,
                                        base=0, pattern=[[-1, P]], channel_multiplier=1)
                nc.gpsimd.affine_select(out=upto[:, :], in_=upto[:, :], compare_op=ALU.is_ge, fill=0.0,
                                        base=0, pattern=[[1, P]], channel_multiplier=-1)
                nc.gpsimd.affine_select(out=after[:, :], in_=after[:, :], compare_op=ALU.is_gt, fill=0.0,
                                        base=0, pattern=[[-1, P]], channel_multiplier=1).then_inc(consts_pool, 1)

            prepare()

            def ffn(stage):
                e = ffn_sems[stage]

                def inverse_std(j, b):
                    s = 2 * j + b
                    pool.wait_ge(e["stats_done"], s + 1)
                    nc.gpsimd.tensor_tensor(rstd[:, b, :], mv[:, b, :, 1], eps_tile[:, :], ALU.add).then_inc(e["var_done"], 1)
                    pool.wait_ge(e["var_done"], s + 1)
                    nc.gpsimd.tensor_tensor(rstd[:, b, :], rstd[:, b, :], minus_half[:, :], ALU.pow).then_inc(e["rstd_done"], 1)

                def key_low(j, b):
                    s = 2 * j + b
                    pool.wait_ge(e["xkhi_done"], s + 1)
                    nc.gpsimd.tensor_tensor(xk_lo[:, :, :], xk[:, :, :], xk_hi[:, :, :].bitcast(F32),
                                            ALU.subtract).then_inc(e["xklo_done"], 1)

                def receptance_low(j, b):
                    s = 2 * j + b
                    pool.wait_ge(e["xrhi_done"], s + 1)
                    nc.gpsimd.tensor_tensor(xr_lo[:, :, :], xr[:, :, :], xr_hi[:, :, :].bitcast(F32),
                                            ALU.subtract).then_inc(e["xrlo_done"], 1)

                def residual(j, b):
                    s = 2 * j + b
                    pool.wait_ge(e["gated_done"], s + 1)
                    t = tiles(b * NT + j * CT, CT)
                    nc.gpsimd.tensor_tensor(t, t, gated, ALU.add).then_inc(e["res_done"], 1)

                for b in range(2):
                    inverse_std(0, b)
                key_low(0, 0)
                receptance_low(0, 0)

                def body(j, first, last):
                    for b in range(2):
                        nj, nb = (j, 1) if b == 0 else (j + 1, 0)
                        if not (first and b == 0):
                            residual(*((j, 0) if b == 1 else (j - 1, 1)))
                        if not last:
                            inverse_std(j + 1, b)
                        if not (last and b == 1):
                            key_low(nj, nb)
                            receptance_low(nj, nb)

                rounds(pool, NJ, body)
                residual(NJ - 1, 1)

            def mem():
                def key_sum(j, b):
                    s = 2 * j + b
                    pool.wait_ge(m["ksq_done"], s + 1)
                    need(pool, m["knorm_done"], s)
                    nc.gpsimd.tensor_tensor(ksum[:, :, :], ksq[:, :, 0:2 * Q], ksq[:, :, 2 * Q:4 * Q], ALU.add).then_inc(m["khalf_done"], 1)
                    pool.wait_ge(m["khalf_done"], s + 1)
                    nc.gpsimd.tensor_tensor(ksum[:, :, 0:Q], ksum[:, :, 0:Q], ksum[:, :, Q:2 * Q], ALU.add).then_inc(m["ksum_done"], 1)

                pool.wait_ge(ffn_sems[0]["xr_done"], NS)
                nc.gpsimd.memset(xnT[:, :, :, 0:1], 0.0).then_inc(shift_zeroed, 1)
                key_sum(0, 0)
                bind_sum(nc.gpsimd, 0, 0, 0)
                bind_sum(nc.gpsimd, 0, 0, 1)

                def body(j, first, last):
                    for b in range(2):
                        nj, nb = (j, 1) if b == 0 else (j + 1, 0)
                        ahead = not (last and b == 1)
                        if ahead:
                            key_sum(nj, nb)
                        ret_sum(nc.gpsimd, j, b, 1)
                        if ahead:
                            bind_sum(nc.gpsimd, nj, nb, 0)
                            bind_sum(nc.gpsimd, nj, nb, 1)

                rounds(pool, NP, body)

            ffn(0)
            mem()
            ffn(1)

        @block.tensor
        def _(pe):
            def fold_bias():
                pe.wait_ge(lnb_folded, 1)
                for f in range(FC):
                    last = nc.tensor.matmul(v_tok[:, 0, :], lnb_rows[:, f, :], wo[:, f, :], start=f == 0, stop=f == FC - 1)
                last.then_inc(lnb_folded, 1)

            def parts(out_ap, high, low, f_high, f_low):
                n = 3 * FC
                k = 0
                for f in range(FC):
                    for w, v in ((high, f_high), (low, f_high), (high, f_low)):
                        last = nc.tensor.matmul(out_ap, w(f), v(f), start=k == 0, stop=k == n - 1)
                        k += 1
                return last

            def ffn(stage):
                e = ffn_sems[stage]

                def transposes(j, b):
                    s = 2 * j + b
                    pe.wait_ge(e["xn_done"], s + 1)
                    need(pe, e["xnT_done"], s)
                    for f in range(FC):
                        for i in range(CT):
                            last = nc.tensor.transpose(xT_ps[:, f, i * P:(i + 1) * P], xn[:, b, i, f * P:(f + 1) * P], ident[:, :])
                    last.then_inc(e["T_done"], 1)

                def key(j, b):
                    s = 2 * j + b
                    pe.wait_ge(e["xklo_done"], s + 1)
                    need(pe, e["relu_done"], 2 * s)
                    for o in range(FC):
                        parts(k_ps[:, o, :],
                              lambda f: wffn_hi[:, 0, f, o * P:(o + 1) * P], lambda f: wffn_lo[:, 0, f, o * P:(o + 1) * P],
                              lambda f: xk_hi[:, f, :], lambda f: xk_lo[:, f, :]).then_inc(e["k_done"], 1)

                def by_token(dst, x_hi, x_lo, w):
                    for i in range(CT):
                        last = parts(dst[:, i, :],
                                     lambda f: x_hi[:, f, i * P:(i + 1) * P], lambda f: x_lo[:, f, i * P:(i + 1) * P],
                                     lambda f: wffn_hi[:, w, f, :], lambda f: wffn_lo[:, w, f, :])
                    return last

                def receptance(j, b):
                    s = 2 * j + b
                    pe.wait_ge(e["xrlo_done"], s + 1)
                    need(pe, e["gate_done"], s)
                    by_token(r_tok, xr_hi, xr_lo, 1).then_inc(e["r_done"], 1)

                def value(j, b):
                    s = 2 * j + b
                    pe.wait_ge(e["kactlo_done"], 2 * s + 2)
                    need(pe, e["gated_done"], s)
                    by_token(v_tok, kact_hi, kact_lo, 2).then_inc(e["v_done"], 1)

                if stage == 1:
                    pe.wait_ge(m["x_done"], MS)
                else:
                    pe.wait_ge(consts_pool, POOL_CONSTS)
                transposes(0, 0)
                pe.wait_ge(weights_ready, 1)

                def body(j, first, last):
                    for b in range(2):
                        if not (last and b == 1):
                            nj, nb = (j, 1) if b == 0 else (j + 1, 0)
                            transposes(nj, nb)
                        key(j, b)
                        if stage == 0 and first and b == 0:
                            fold_bias()
                        receptance(j, b)
                        if stage == 0 and first and b == 0:
                            pe.wait_ge(mem_ready, 1)
                        value(j, b)

                rounds(pe, NJ, body)

            def mem():
                def transposes(j, b):
                    s = 2 * j + b
                    pe.wait_ge(m["xn_done"], s + 1)
                    need(pe, m["xnT_done"], s)
                    need(pe, m["normedT_done"], s - 2)
                    for f in range(FC):
                        for i in range(2):
                            last = nc.tensor.transpose(t_bank[:, f, i * P:(i + 1) * P], m_xn[:, i, f * P:(f + 1) * P], ident[:, :])
                    last.then_inc(m["T_done"], 1)

                def project(dst, col, done):
                    for i in range(2):
                        for f in range(FC):
                            nc.tensor.matmul(dst[:, i, :], m_xnT[:, f, i * P:(i + 1) * P], wkv[:, f, col:col + D],
                                             start=f == 0, stop=False)
                        last = nc.tensor.matmul(dst[:, i, :], ones[:, :], bias3[:, col:col + D], start=False, stop=True)
                    last.then_inc(done, 1)

                def project_keys(j, b):
                    s = 2 * j + b
                    pe.wait_ge(m["xnT_done"], s + 1)
                    need(pe, m["khat_done"], s - 1)
                    project(keys[b], 0, m["K_done"])

                def project_values(j, b):
                    s = 2 * j + b
                    need(pe, bprod_done[1], s - 1)
                    project(values[b], D, m["V_done"])

                def sum_upto(j, b, i):
                    s = 2 * j + b
                    pe.wait_ge(bound_done[i], s + 1)
                    nc.tensor.matmul(memory[b], upto[:, :], bound[:, i, :], start=False, stop=True,
                                     skip_group_check=True).then_inc(upto_done[i], 1)

                def sum_after(j, b, i):
                    s = 2 * j + b
                    pe.wait_ge(rprod_done[i], s + 1)
                    nc.tensor.matmul(memory[b], after[:, :], bound[:, i, :], start=False, stop=True,
                                     skip_group_check=True).then_inc(after_done[i], 1)

                def ret_transposes(j, b):
                    s = 2 * j + b
                    pe.wait_ge(m["normed_done"], s + 1)
                    behind = s + 3 if not isinstance(s, int) else min(s + 3, MS)
                    pe.wait_ge(m["xnT_done"], behind)
                    for f in range(FC):
                        for i in range(2):
                            last = nc.tensor.transpose(t_bank[:, f, i * P:(i + 1) * P], normed[:, i, f * P:(f + 1) * P], ident[:, :])
                    last.then_inc(m["nT_done"], 1)

                def output(j, b):
                    s = 2 * j + b
                    pe.wait_ge(m["normedT_done"], s + 1)
                    need(pe, m["x_done"], s)
                    for i in range(2):
                        for f in range(FC):
                            nc.tensor.matmul(o_bank[:, i, :], normedT[:, f, i * P:(i + 1) * P], wo[:, f, :],
                                             start=f == 0, stop=False)
                        last = nc.tensor.matmul(o_bank[:, i, :], ones[:, :], bias3[:, 2 * D:], start=False, stop=True)
                    last.then_inc(m["O_done"], 1)

                pe.wait_ge(ffn_sems[0]["gated_done"], NS)
                for b in range(2):
                    nc.tensor.matmul(memory[b], upto[:, :], zeros[:, :], start=True, stop=True, skip_group_check=True)
                transposes(0, 0)
                project_keys(0, 0)
                project_values(0, 0)
                transposes(0, 1)

                def body(j, first, last):
                    for b in range(2):
                        nj, nb = (j, 1) if b == 0 else (j + 1, 0)
                        pj, pb = (j, 0) if b == 1 else (j - 1, 1)
                        ahead, behind = not (last and b == 1), not (first and b == 0)
                        sum_upto(j, b, 0)
                        if ahead:
                            project_keys(nj, nb)
                        sum_after(j, b, 0)
                        sum_upto(j, b, 1)
                        if ahead:
                            project_values(nj, nb)
                        if behind:
                            ret_transposes(pj, pb)
                        if not last:
                            transposes(j + 1, b)
                        if behind:
                            output(pj, pb)
                        sum_after(j, b, 1)

                rounds(pe, NP, body)
                ret_transposes(NP - 1, 1)
                output(NP - 1, 1)

            ffn(0)
            mem()
            ffn(1)


POOL_CONSTS = 2


def kernel(L0_attn_x, L0_attn_Wk, L0_attn_bk, L0_attn_Wv, L0_attn_bv, L0_attn_ln_g, L0_attn_ln_b, L0_attn_Wo, L0_attn_bo,
           L0_ffn_W_r, L0_ffn_W_k, L0_ffn_W_v, L0_ffn_mu_r, L0_ffn_mu_k):
    import numpy as np
    import concourse.bacc as bacc
    from concourse.bass_utils import run_bass_kernel_spmd

    def by_component(a):
        a = np.asarray(a)
        return a.reshape(a.shape[0] // 4, 4, -1).transpose(1, 0, 2).reshape(a.shape)

    arrays = {
        "x": np.asarray(L0_attn_x),
        "w_kv": np.concatenate([by_component(L0_attn_Wk).T, by_component(L0_attn_Wv).T], axis=1),
        "w_o": by_component(np.asarray(L0_attn_Wo).T),
        "w_r": np.asarray(L0_ffn_W_r).T,
        "w_k": np.asarray(L0_ffn_W_k).T,
        "w_v": np.asarray(L0_ffn_W_v).T,
        "b_kv": np.concatenate([by_component(L0_attn_bk), by_component(L0_attn_bv)]),
        "b_o": np.asarray(L0_attn_bo),
        "columns": np.concatenate([v.reshape(-1, P).T for v in (np.asarray(L0_ffn_mu_r), np.asarray(L0_ffn_mu_k),
                                                                by_component(L0_attn_ln_g), by_component(L0_attn_ln_b))], axis=1),
    }
    arrays = {name: np.ascontiguousarray(a) for name, a in arrays.items()}
    nc = bacc.Bacc("TRN2", target_bir_lowering=False, num_devices=1)
    args = [nc.dram_tensor(name, a.shape, mybir.dt.from_np(a.dtype), kind="ExternalInput").ap() for name, a in arrays.items()]
    out = nc.dram_tensor("out", arrays["x"].shape, F32, kind="ExternalOutput").ap()
    macaron(nc, *args, out)
    r = run_bass_kernel_spmd(nc, [arrays], core_ids=[0])
    return r.results[0]["out"]
```

```python
from contextlib import ExitStack

import concourse.bass as bass
from concourse import mybir

F32 = mybir.dt.float32
F32R = mybir.dt.float32r
BF16 = mybir.dt.bfloat16
I32 = mybir.dt.int32
ALU = mybir.AluOpType
ACT = mybir.ActivationFunctionType

P = 128
LN_EPS = 1e-5
NORM_EPS = 1e-12
STAT = 6


def need(engine, semaphore, count):
    if isinstance(count, int) and count <= 0:
        return
    engine.wait_ge(semaphore, count)


def rounds(engine, n, before, peel, body):
    def has(done, left):
        return lambda b, d: b + d >= -2 * done and b + d < 2 * (left + 1)

    for done in range(before):
        body(done, has(done, peel))
    with engine.Fori(before, n - peel) as j:
        body(j, has(before, peel))
    for left in reversed(range(peel)):
        body(n - 1 - left, has(n, left))


def at(j, b, d):
    return j + (b + d) // 2, (b + d) % 2


def macaron(nc, x, w_kv, w_o, w_r, w_k, w_v, columns, out):
    B, L, D = x.shape
    FC = D // P
    NT = L // P
    Q = D // 4
    CT = 4
    DT = 3
    CW = CT * P
    NJ = NT // CT
    NP = NT // 2
    NS = B * NJ
    MS = B * NP
    assert B == 2 and D == 2 * P and L % CW == 0

    with ExitStack() as ctx:
        def sb(name, shape, dt=F32):
            return ctx.enter_context(nc.sbuf_tensor(name, shape, dt))

        def sem(name):
            return ctx.enter_context(nc.semaphore(name))

        res = sb("res", [P, B * NT * D])
        wkv = sb("wkv", [P, FC, 2 * D])
        wo = sb("wo", [P, FC, D])
        wffn = sb("wffn", [P, 3, FC, D])
        wffn_hi = sb("wffn_hi", [P, 3, FC, D], F32R)
        wffn_lo = sb("wffn_lo", [P, 3, FC, D], F32R)
        cols = sb("cols", [P, 7 * FC])
        mur, muk, lng, lnb = (cols[:, i * FC:(i + 1) * FC] for i in range(4))
        bias = cols[:, 4 * FC:]
        bias_rest = sb("bias_rest", [P, 3 * FC])
        bias_part = sb("bias_part", [P, 2, 3 * FC], BF16)
        bias_lines = sb("bias_lines", [P, 3 * FC, P])
        bias3 = sb("bias3", [P, 3 * D], BF16)
        ones = sb("ones", [P, P], BF16)
        ident = sb("ident", [P, P])
        upto = sb("upto", [P, P])
        after = sb("after", [P, P])
        zeros = sb("zeros", [P, D])
        pos = sb("pos", [P, NT], I32)
        eps4 = sb("eps4", [P, NP, 4])
        minus_half = sb("minus_half", [P, CT])
        eps_tile = sb("eps_tile", [P, CT])
        spare = sb("spare", [P, 1])
        spare_act = sb("spare_act", [P, 1])

        st = sb("st", [P, 2, CT, STAT])
        mv = sb("mv", [P, 2, CT, 2])
        rstd = sb("rstd", [P, 2, CT])
        shift = sb("shift", [P, 2, CT])
        xn = sb("xn", [P, 2, CT, D])
        xnT = sb("xnT", [P, 2, FC, CW + 1])
        diff = sb("diff", [P, FC, CW])
        xk = sb("xk", [P, FC, CW])
        xk_hi = sb("xk_hi", [P, FC, CW], F32R)
        xk_lo = sb("xk_lo", [P, FC, CW], F32R)
        xr = sb("xr", [P, FC, CW])
        xr_hi = sb("xr_hi", [P, FC, CW], F32R)
        xr_lo = sb("xr_lo", [P, FC, CW], F32R)
        relu_k = sb("relu_k", [P, FC, CW])
        kact = sb("kact", [P, FC, CW])
        kact_hi = sb("kact_hi", [P, FC, CW], F32R)
        kact_lo = sb("kact_lo", [P, FC, CW], F32R)
        gating_buffers = sb("gating_buffers", [P, 2, CT * D])
        gate, gated = (gating_buffers[:, i, :].rearrange("p (t n) -> p t n", n=D) for i in range(2))

        n_st = sb("n_st", [P, 2, 4, STAT])
        n_mv = sb("n_mv", [P, 2, 4, 2])
        n_var = sb("n_var", [P, 2, 4])
        n_std = sb("n_std", [P, 2, 4])
        n_rstd = sb("n_rstd", [P, 2, 4])
        n_shift = sb("n_shift", [P, 2, 4])
        n_gain = sb("n_gain", [P, 2, 2])
        m_xn = sb("m_xn", [P, 2, D])
        m_xnT = sb("m_xnT", [P, FC, 2 * P])
        ksq = sb("ksq", [P, 2, D])
        ksum = sb("ksum", [P, 2, 2 * Q])
        knorm = sb("knorm", [P, 2, Q])
        kinv = sb("kinv", [P, 2, Q])
        khat = sb("khat", [P, 2, 2, D])
        bprod = xn[:, :, :, :].rearrange("p i t (c n) -> p i (t c) n", n=Q)
        rprod = gating_buffers[:, :, :].rearrange("p i (c n) -> p i c n", n=Q)
        bhalf = sb("bhalf", [P, 2, 2, 4, Q])
        rhalf = sb("rhalf", [P, 2, 2, 4, Q])
        bound = kact[:, :, :].rearrange("p b (t n) -> p b t n", n=D)
        ret = sb("ret", [P, 2, 2, D])
        normed = sb("normed", [P, 2, D])
        normedT = sb("normedT", [P, FC, 2 * P])

        bank = [ctx.enter_context(nc.psum_tensor(f"bank{i}", [P, 2, 512], F32)) for i in range(4)]
        k_ps, v_ps = bank[1][:, :, :], bank[3][:, :, :]
        transpose_banks, receptance_banks = ([bank[i][:, :, :], bank[2 - i][:, :, :]] for i in (0, 2))
        v_flat = v_ps.rearrange("p h n -> p (h n)")
        v_tok = v_ps.rearrange("p h (t n) -> p (h t) n", n=D)
        t_bank = bank[0][:, 0, :].rearrange("p (f t) -> p f t", f=FC)
        o_bank = bank[0][:, 1, :].rearrange("p (t n) -> p t n", t=2)
        keys = bank[1][:, 0, :].rearrange("p (t n) -> p t n", t=2)
        rt_bank = bank[1][:, 1, :].rearrange("p (f t) -> p f t", f=FC)
        values = [bank[2][:, b, :].rearrange("p (t n) -> p t n", t=2) for b in range(2)]
        memory = [bank[3][:, b, 0:D] for b in range(2)]

        def tiles(tile, n):
            return res[:, bass.ds(tile * D, n * D)].rearrange("p (t n) -> p t n", n=D)

        def rows(dram, b, j, n):
            return dram[b, bass.ds(j * (n * P), n * P), :].rearrange("(t p) n -> p t n", p=P)

        consts_in = sem("consts_in")
        wo_in = sem("wo_in")
        wkv_in = sem("wkv_in")
        consts_pool = sem("consts_pool")
        setup = sem("setup")
        lnb_folded = sem("lnb_folded")
        bias_lines_ready = sem("bias_lines_ready")
        bias_rows_ready = sem("bias_rows_ready")
        weights_ready = sem("weights_ready")
        mem_ready = sem("mem_ready")
        shift_zeroed = sem("shift_zeroed")
        table_loaded = sem("table_loaded")
        last_done = sem("last_done")
        x_in = [sem(f"x_in{b}") for b in range(2)]
        x_out = [sem(f"x_out{b}") for b in range(2)]

        FFN_SEMS = ["st_done", "stats_done", "var_done", "rstd_done", "shift_done", "xn_done", "xn_act_done", "T_done", "carry_done", "xnT_done",
                    "diff_done", "xk_done", "xkhi_done", "xklo_done", "xr_done", "xrhi_done", "xrlo_done", "k_done",
                    "relu_done", "kact_done", "kacthi_done", "kactlo_done", "r_done", "gate_done", "v_done", "gated_done",
                    "res_done"]
        ffn_sems = [{n: sem(f"f{i}_{n}") for n in FFN_SEMS} for i in range(2)]
        MEM_SEMS = ["st_done", "st_ret_done", "mv_done", "var_done", "std_done", "rstd_done", "scales_done", "xn_done", "T_done", "xnT_done",
                    "res_done", "K_done", "V_done", "ksq_done", "khalf_done", "ksum_done", "knorm_done", "kmax_done",
                    "kinv_done", "khat_done", "normed_done", "nT_done", "normedT_done", "O_done", "x_done"]
        m = {n: sem(f"m_{n}") for n in MEM_SEMS}

        def for_tiles(name):
            return [sem(f"m_{name}{i}_done") for i in range(2)]

        bprod_done, bhalf_done, bound_done = for_tiles("bprod"), for_tiles("bhalf"), for_tiles("bound")
        rprod_done, rhalf_done, ret_done = for_tiles("rprod"), for_tiles("rhalf"), for_tiles("ret")
        upto_done, after_done = for_tiles("upto"), for_tiles("after")

        def capped(count):
            return min(count, MS) if isinstance(count, int) else count

        def x_ready(engine, stage, b, j):
            if stage == 0:
                engine.wait_ge(x_in[b], 16 * (j + 1))
            else:
                engine.wait_ge(m["x_done"], CT * j + b + CT // 2 + 1)

        block = ctx.enter_context(nc.Block())

        def additions(engine, operations, done):
            for o, a, b, op in operations:
                last = engine.tensor_tensor(o, a, b, op)
            last.then_inc(done, 1)

        def bind_sum(engine, j, b, i):
            bind_halves(engine, j, b, i)
            bind_total(engine, j, b, i)

        def bind_halves(engine, j, b, i):
            s = 2 * j + b
            engine.wait_ge(bprod_done[i], s + 1)
            need(engine, bound_done[i], s)
            p, ha, hq = bprod[:, i, :, :], bhalf[:, i, 0, :, :], bhalf[:, i, 1, :, :]
            additions(engine,
                   [(ha[:, 0:3:2, :], p[:, 0:3:2, :], p[:, 5:8:2, :], ALU.subtract),
                    (ha[:, 1:4:2, :], p[:, 1:4:2, :], p[:, 4:7:2, :], ALU.add),
                    (hq[:, 0:3:2, :], p[:, 10:14:3, :], p[:, 15:7:-7, :], ALU.add),
                    (hq[:, 1:4:2, :], p[:, 11:13:1, :], p[:, 14:8:-5, :], ALU.subtract)],
                   bhalf_done[i])

        def bind_total(engine, j, b, i):
            s = 2 * j + b
            engine.wait_ge(bhalf_done[i], s + 1)
            need(engine, after_done[i], s - 1)
            ha, hq = bhalf[:, i, 0, :, :], bhalf[:, i, 1, :, :]
            out4 = bound[:, b, i, :].rearrange("p (c n) -> p c n", n=Q)
            additions(engine,
                   [(out4[:, 0:1, :], ha[:, 0:1, :], hq[:, 0:1, :], ALU.subtract),
                    (out4[:, 1:4, :], ha[:, 1:4, :], hq[:, 1:4, :], ALU.add)],
                   bound_done[i])

        def ret_sum(engine, j, b, i):
            ret_halves(engine, j, b, i)
            ret_total(engine, j, b, i)

        def ret_halves(engine, j, b, i):
            s = 2 * j + b
            engine.wait_ge(rprod_done[i], s + 1)
            need(engine, ret_done[i], s)
            p, ha, hq = rprod[:, i, :, :], rhalf[:, i, 0, :, :], rhalf[:, i, 1, :, :]
            additions(engine,
                   [(ha[:, 0:1, :], p[:, 0:1, :], p[:, 5:6, :], ALU.add),
                    (ha[:, 1:4, :], p[:, 4:13:4, :], p[:, 1:4, :], ALU.subtract),
                    (hq[:, 0:1, :], p[:, 10:11, :], p[:, 15:16, :], ALU.add),
                    (hq[:, 1:4:2, :], p[:, 14:8:-5, :], p[:, 11:5:-5, :], ALU.subtract),
                    (hq[:, 2:3, :], p[:, 7:8, :], p[:, 13:14, :], ALU.subtract)],
                   rhalf_done[i])

        def ret_total(engine, j, b, i):
            s = 2 * j + b
            engine.wait_ge(rhalf_done[i], s + 1)
            need(engine, m["normed_done"], s - 1)
            additions(engine, [(ret[:, b, i, :], rhalf[:, i, 0, :, :].rearrange("p c n -> p (c n)"),
                                rhalf[:, i, 1, :, :].rearrange("p c n -> p (c n)"), ALU.add)], ret_done[i])

        def key_low(engine, ops, e, j, b):
            s = 2 * j + b
            engine.wait_ge(e["xkhi_done"], s + 1)
            ops.tensor_tensor(xk_lo[:, :, :], xk[:, :, :], xk_hi[:, :, :].bitcast(F32),
                              ALU.subtract).then_inc(e["xklo_done"], 1)

        @block.sync
        def _(sp):
            def load_x(b, j):
                sp.dma_start(tiles(b * NT + j * CT, CT), rows(x, b, j, CT)).then_inc(x_in[b], 16)

            load_x(0, 0)
            sp.dma_start(cols[:, :], columns).then_inc(consts_in, 16)
            for i, w in enumerate((w_k, w_r, w_v)):
                sp.dma_start(wffn[:, i, :, :], w.rearrange("(f p) n -> p f n", p=P)).then_inc(consts_in, 16)
            load_x(1, 0)
            sp.dma_start(wo[:, :, :], w_o.rearrange("(f p) n -> p f n", p=P)).then_inc(wo_in, 16)
            sp.dma_start(wkv[:, :, :], w_kv.rearrange("(f p) n -> p f n", p=P)).then_inc(wkv_in, 16)
            with sp.Fori(1, NJ) as j:
                for b in range(2):
                    sp.wait_ge(x_in[b], 16 * j)
                    load_x(b, j)
            done = ffn_sems[1]["res_done"]

            def store(j, b):
                sp.wait_ge(done, 2 * j + b + 1)
                sp.dma_start(rows(out, b, j, CT), tiles(b * NT + j * CT, CT)).then_inc(x_out[b], 16)

            with sp.Fori(0, NJ - 1) as j:
                for b in range(2):
                    store(j, b)
            store(NJ - 1, 0)
            for h in range(2):
                sp.wait_ge(last_done, h + 1)
                sp.dma_start(rows(out, 1, 2 * NJ - 2 + h, CT // 2),
                             tiles(2 * NT - CT + h * CT // 2, CT // 2)).then_inc(x_out[1], 16)
            sp.wait_ge(x_out[0], 16 * NJ)
            sp.wait_ge(x_out[1], 16 * (NJ + 1))

        @block.vector
        def _(dve):
            own_steps = 0

            def own(instruction):
                nonlocal own_steps
                own_steps += 1
                instruction.then_inc(setup, 1)
                dve.wait_ge(setup, own_steps)

            def split_weights_high():
                dve.wait_ge(consts_in, 16 * 4)
                own(nc.vector.tensor_scalar(wffn[:, 2, :, :], wffn[:, 2, :, :], 0.5, None, ALU.mult))
                own(nc.vector.tensor_copy(wffn_hi[:, :, :, :], wffn[:, :, :, :]))

            def split_weights_low(first, end):
                nc.vector.tensor_tensor(wffn_lo[:, first:end, :, :], wffn[:, first:end, :, :],
                                        wffn_hi[:, first:end, :, :].bitcast(F32), ALU.subtract).then_inc(weights_ready, 1)

            def prepare_memory():
                dve.wait_ge(lnb_folded, 1)
                own(nc.vector.tensor_tensor(bias[:, 2 * FC:], v_ps[:, 0, 0:FC], bias[:, 2 * FC:], ALU.add))
                own(nc.vector.tensor_copy(bias_part[:, 0, :], bias))
                nc.vector.tensor_copy(bias_lines[:, :, 0], bias_part[:, 0, :])
                own(nc.vector.tensor_tensor(bias_rest[:, :], bias, bias_part[:, 0, :], ALU.subtract))
                own(nc.vector.tensor_copy(bias_part[:, 1, :], bias_rest[:, :]))
                nc.vector.tensor_copy(bias_lines[:, :, 32], bias_part[:, 1, :])
                nc.vector.tensor_tensor(bias_lines[:, :, 64], bias_rest[:, :], bias_part[:, 1, :],
                                        ALU.subtract).then_inc(bias_lines_ready, 1)
                for f in range(FC):
                    nc.vector.tensor_scalar(wo[:, f, :], wo[:, f, :], lng[:, f:f + 1], None, ALU.mult)
                nc.vector.tensor_scalar(eps4[:, :, 0:2], pos[:, :].rearrange("p (j i) -> p j i", i=2), LN_EPS, None, ALU.mult)
                nc.vector.memset(eps4[:, :, 2:4], LN_EPS).then_inc(mem_ready, 1)

            def ffn(stage):
                e = ffn_sems[stage]
                xT_ps = transpose_banks[stage]
                r_tok = receptance_banks[stage].rearrange("p h (t n) -> p (h t) n", n=D)

                def stats(j, b):
                    x_ready(dve, stage, b, j)
                    t = tiles(b * NT + j * CT, CT)
                    for i in range(CT):
                        last = nc.vector.bn_stats(st[:, b, i, :], t[:, i, :])
                    last.then_inc(e["st_done"], 1)

                def aggregate(j, b):
                    for i in range(CT):
                        last = nc.vector.bn_aggr(mv[:, b, i, :], st[:, b, i, :])
                    last.then_inc(e["stats_done"], 1)

                def normalize(j, b):
                    s = 2 * j + b
                    dve.wait_ge(e["rstd_done"], s + 1)
                    need(dve, e["T_done"], s - 1)
                    nc.vector.scalar_tensor_tensor(shift[:, b, DT:], mv[:, b, DT:, 0], -1.0, rstd[:, b, DT:],
                                                   ALU.mult, ALU.mult).then_inc(e["shift_done"], 1)
                    t = tiles(b * NT + j * CT, CT)
                    for i in range(DT):
                        last = nc.vector.tensor_scalar(xn[:, b, i, :], t[:, i, :], mv[:, b, i, 0:1], rstd[:, b, i:i + 1],
                                                       ALU.subtract, ALU.mult)
                    last.then_inc(e["xn_done"], 1)

                def difference(j, b):
                    s = 2 * j + b
                    dve.wait_ge(e["xnT_done"], s + 1)
                    need(dve, e["xr_done"], FC * s)
                    nc.vector.tensor_tensor(diff[:, :, :], xnT[:, b, :, 1:CW + 1], xnT[:, b, :, 0:CW],
                                            ALU.subtract).then_inc(e["diff_done"], 1)

                def mix(j, b, f, dst, mu, read, done):
                    s = 2 * j + b
                    dve.wait_ge(e["diff_done"], s + 1)
                    for semaphore in read:
                        need(dve, e[semaphore], s)
                    nc.vector.scalar_tensor_tensor(dst[:, f, :], diff[:, f, :], mu[:, f:f + 1], xnT[:, b, f, 0:CW],
                                                   ALU.mult, ALU.add).then_inc(e[done], 1)

                def square_low(j, b, o):
                    s = 2 * j + b
                    dve.wait_ge(e["kacthi_done"], 2 * s + o + 1)
                    nc.vector.tensor_tensor(kact_lo[:, o, :], kact[:, o, :], kact_hi[:, o, :].bitcast(F32),
                                            ALU.subtract).then_inc(e["kactlo_done"], 1)

                def gating(j, b):
                    s = 2 * j + b
                    dve.wait_ge(e["gate_done"], s + 1)
                    dve.wait_ge(e["v_done"], 2 * (s + 1))
                    need(dve, e["res_done"], s)
                    nc.vector.tensor_tensor(gated, v_tok, gate, ALU.mult).then_inc(e["gated_done"], 1)

                def mix_key(j, b, f):
                    mix(j, b, f, xk, muk, ["xkhi_done", "xklo_done"], "xk_done")

                def mix_receptance(j, b, f):
                    mix(j, b, f, xr, mur, ["xrhi_done", "xrlo_done"], "xr_done")

                def own_wait(s):
                    dve.wait_ge(e["st_done"], s + 1)
                    nc.vector.memset(spare[:, :], 0.0)

                def stats_of(j, b):
                    stats(j, b)
                    own_wait(2 * j + b)
                    aggregate(j, b)

                def first_mix(meanwhile):
                    difference(0, 0)
                    mix_key(0, 0, 0)
                    mix_key(0, 0, 1)
                    meanwhile()
                    mix_receptance(0, 0, 0)
                    mix_receptance(0, 0, 1)
                    key_low(dve, nc.vector, e, 0, 0)

                def body(j, has):
                    for b in range(2):
                        nj, nb = at(j, b, 1)
                        mixing = has(b, 1)
                        first = not has(b, -1)
                        if has(b, 2) and not first:
                            normalize(j + 1, b)
                        if has(b, -1):
                            gating(*at(j, b, -1))
                        if mixing:
                            difference(nj, nb)
                            mix_key(nj, nb, 0)
                            mix_key(nj, nb, 1)
                        if first:
                            normalize(1, 0)
                            stats_of(1, 1)
                        square_low(j, b, 0)
                        square_low(j, b, 1)
                        if mixing:
                            mix_receptance(nj, nb, 0)
                            mix_receptance(nj, nb, 1)
                        if has(b, 4):
                            stats_of(j + 2, b)

                def steps():
                    rounds(dve, NJ, 1, 2, body)

                def last_gating():
                    gating(NJ - 1, 1)

                def last_blocks():
                    dve.wait_ge(e["gate_done"], NS)
                    dve.wait_ge(e["res_done"], NS - 1)
                    for h in range(2):
                        span = slice(h * CT // 2, (h + 1) * CT // 2)
                        dve.wait_ge(e["v_done"], 2 * (NS - 1) + h + 1)
                        nc.vector.tensor_tensor(gated[:, span, :], v_tok[:, span, :], gate[:, span, :],
                                                ALU.mult).then_inc(e["gated_done"], 1)
                        dve.wait_ge(e["gated_done"], NS + h)
                        t = tiles(2 * NT - CT + h * CT // 2, CT // 2)
                        nc.vector.tensor_tensor(t, t, gated[:, span, :], ALU.add).then_inc(last_done, 1)

                return stats_of, normalize, first_mix, steps, last_gating, last_blocks

            def mem():
                def ln_stats_res(r, ret_at, res_at):
                    if res_at is not None:
                        jj, q = res_at
                        need(dve, m["res_done"], capped(r - 1))
                        t = tiles(q * NT + jj * 2, 2)
                        for i in range(2):
                            nc.vector.bn_stats(n_st[:, q, 2 + i, :], t[:, i, :]).then_inc(m["st_done"], 1)

                def ln_stats_ret(r, ret_at, res_at):
                    if ret_at is not None:
                        need(dve, m["res_done"], capped(r - 1))
                        need(dve, m["normed_done"], r - 5)
                        pj, q = ret_at
                        for i in range(2):
                            dve.wait_ge(ret_done[i], r - 3)
                            nc.vector.bn_stats(n_st[:, q, i, :], ret[:, q, i, :]).then_inc(m["st_ret_done"], 1)

                def own_stats(r, ret_at, res_at):
                    if res_at is not None:
                        dve.wait_ge(m["st_done"], 2 * (r + 1))
                    if ret_at is not None:
                        dve.wait_ge(m["st_ret_done"], 2 * (r - 3))

                def ln_span(ret_at, res_at):
                    return (ret_at or res_at)[1], (0 if ret_at is not None else 2), (4 if res_at is not None else 2)

                def ln_moments(r, ret_at, res_at):
                    q, lo, hi = ln_span(ret_at, res_at)
                    for i in range(lo, hi):
                        last = nc.vector.bn_aggr(n_mv[:, q, i, :], n_st[:, q, i, :])
                    last.then_inc(m["mv_done"], 1)

                def ln_variance(r, ret_at, res_at):
                    q, lo, hi = ln_span(ret_at, res_at)
                    dve.wait_ge(m["mv_done"], r + 1)
                    pj = ret_at[0] if ret_at is not None else 0
                    nc.vector.tensor_tensor(n_var[:, q, lo:hi], n_mv[:, q, lo:hi, 1],
                                            eps4[:, bass.ds(pj, 1), lo:hi].rearrange("p j i -> p (j i)"), ALU.add).then_inc(m["var_done"], 1)

                def ln_inverse(r, ret_at, res_at):
                    q, lo, hi = ln_span(ret_at, res_at)
                    dve.wait_ge(m["std_done"], r + 1)
                    nc.vector.reciprocal(n_rstd[:, q, lo:hi], n_std[:, q, lo:hi]).then_inc(m["rstd_done"], 1)

                def ln_scales(r, ret_at, res_at):
                    q, lo, hi = ln_span(ret_at, res_at)
                    dve.wait_ge(m["rstd_done"], r + 1)
                    if res_at is not None:
                        nc.vector.tensor_scalar(n_gain[:, q, :], n_rstd[:, q, 2:4], 1.0, None, ALU.add)
                    nc.vector.scalar_tensor_tensor(n_shift[:, q, lo:hi], n_mv[:, q, lo:hi, 0], -1.0, n_rstd[:, q, lo:hi],
                                                   ALU.mult, ALU.mult).then_inc(m["scales_done"], 1)

                def ln_all(r, ret_at, res_at):
                    for step in (ln_moments, ln_variance, ln_inverse, ln_scales):
                        step(r, ret_at, res_at)

                def key_max(j, b):
                    dve.wait_ge(m["knorm_done"], 2 * j + b + 1)
                    nc.vector.tensor_scalar(knorm[:, :, :], knorm[:, :, :], NORM_EPS, None, ALU.max).then_inc(m["kmax_done"], 1)

                def key_inverse(j, b):
                    s = 2 * j + b
                    dve.wait_ge(m["kmax_done"], s + 1)
                    need(dve, m["khat_done"], s)
                    nc.vector.reciprocal(kinv[:, :, :], knorm[:, :, :]).then_inc(m["kinv_done"], 1)

                def key_unit(j, b):
                    s = 2 * j + b
                    dve.wait_ge(m["kinv_done"], s + 1)
                    dve.wait_ge(m["ksq_done"], s + 1)
                    need(dve, rprod_done[1], s - 1)
                    nc.vector.tensor_tensor(khat[:, b, :, :].rearrange("p t (c n) -> p t c n", n=Q),
                                            keys.rearrange("p t (c n) -> p t c n", n=Q),
                                            kinv[:, :, :].unsqueeze(2).to_broadcast([P, 2, 4, Q]), ALU.mult).then_inc(m["khat_done"], 1)

                def all_products(dst, b, i, of, done):
                    nc.vector.tensor_tensor(
                        dst[:, i, :, :].rearrange("p (a b) n -> p a b n", a=4),
                        of.rearrange("p (a n) -> p a n", n=Q).unsqueeze(2).to_broadcast([P, 4, 4, Q]),
                        khat[:, b, i, :].rearrange("p (b n) -> p b n", n=Q).unsqueeze(1).to_broadcast([P, 4, 4, Q]),
                        ALU.mult).then_inc(done, 1)

                def bind(j, b, i):
                    s = 2 * j + b
                    dve.wait_ge(m["khat_done"], s + 1)
                    dve.wait_ge(m["V_done"], s + 1)
                    need(dve, bound_done[i], s)
                    all_products(bprod, b, i, values[b][:, i, :], bprod_done[i])

                def retrieve(j, b, i):
                    s = 2 * j + b
                    need(dve, ret_done[i], s)
                    dve.wait_ge(upto_done[i], s + 1)
                    all_products(rprod, b, i, memory[b], rprod_done[i])

                def first_layernorms(start, end):
                    dve.wait_ge(ffn_sems[0]["res_done"], B)
                    for r in range(start, end):
                        where = None, (r // 2, r % 2)
                        ln_stats_res(r, *where)
                        own_stats(r, *where)
                        ln_all(r, *where)

                def first_bind():
                    key_max(0, 0)
                    key_inverse(0, 0)
                    key_unit(0, 0)
                    bind(0, 0, 0)
                    bind(0, 0, 1)
                    key_max(0, 1)
                    key_inverse(0, 1)
                    dve.wait_ge(ffn_sems[0]["res_done"], NS)

                def body(j, has, start_last, amid_last):
                    for b in range(2):
                        s = 2 * j + b
                        if not has(b, 1):
                            start_last()
                        where = at(j, b, -1) if has(b, -1) else None, at(j, b, 3) if has(b, 3) else None
                        if has(b, 1):
                            key_unit(*at(j, b, 1))
                        ln_stats_res(s + 3, *where)
                        if has(b, 1):
                            bind(*at(j, b, 1), 0)
                        retrieve(j, b, 0)
                        ln_stats_ret(s + 3, *where)
                        own_stats(s + 3, *where)
                        if has(b, 1):
                            bind(*at(j, b, 1), 1)
                        ln_moments(s + 3, *where)
                        ret_halves(nc.vector, j, b, 0)
                        ln_variance(s + 3, *where)
                        ret_total(nc.vector, j, b, 0)
                        ln_inverse(s + 3, *where)
                        if has(b, 2):
                            key_max(j + 1, b)
                        if not has(b, 1):
                            amid_last()
                        retrieve(j, b, 1)
                        ln_scales(s + 3, *where)
                        if has(b, 2):
                            key_inverse(j + 1, b)

                def steps(start_last, amid_last):
                    rounds(dve, NP, 2, 2, lambda j, has: body(j, has, start_last, amid_last))

                def last_layernorm():
                    where = (NP - 1, 1), None
                    ln_stats_ret(MS + 3, *where)
                    own_stats(MS + 3, *where)
                    ln_all(MS + 3, *where)

                return first_layernorms, first_bind, steps, last_layernorm

            stats_of, normalize, first_mix, ffn_steps, last_gating, _ = ffn(0)
            first_layernorms, first_bind, mem_steps, last_layernorm = mem()
            nc.vector.memset(ones[:, :], 1.0)
            stats_of(0, 0)
            split_weights_high()
            normalize(0, 0)
            split_weights_low(0, 1)
            stats_of(0, 1)

            def before_receptance():
                normalize(0, 1)
                prepare_memory()

            first_mix(before_receptance)
            split_weights_low(1, 3)
            stats_of(1, 0)
            ffn_steps()
            first_layernorms(0, 1)
            last_gating()
            first_layernorms(1, 3)
            first_bind()
            stats_of, normalize, first_mix, ffn_steps, _, last_blocks = ffn(1)

            def first_stats():
                stats_of(0, 0)
                stats_of(0, 1)

            def first_normalize():
                normalize(0, 0)
                normalize(0, 1)

            mem_steps(first_stats, first_normalize)
            first_mix(last_layernorm)
            stats_of(1, 0)
            ffn_steps()
            last_blocks()

        @block.scalar
        def _(act):
            tables = 0

            def load_table(function):
                nonlocal tables
                need(act, table_loaded, tables)
                nc.scalar.activation(spare_act[:, :], eps_tile[:, 0:1], function).then_inc(table_loaded, 1)
                tables += 1

            def ffn(stage):
                e = ffn_sems[stage]
                xT_ps = transpose_banks[stage]
                r_tok = receptance_banks[stage].rearrange("p h (t n) -> p (h t) n", n=D)

                def evict_xT(j, b, first):
                    s = 2 * j + b
                    act.wait_ge(e["T_done"], s + 1)
                    need(act, e["xr_done"], FC * (s - 1))
                    if not first:
                        nc.scalar.copy(xnT[:, b, :, 0:1], xnT[:, b, :, CW:CW + 1]).then_inc(e["carry_done"], 1)
                        act.wait_ge(e["carry_done"], s - 1)
                    nc.scalar.copy(xnT[:, b, :, 1:CW + 1], xT_ps).then_inc(e["xnT_done"], 1)

                def normalize(j, b):
                    s = 2 * j + b
                    act.wait_ge(e["shift_done"], s + 1)
                    t = tiles(b * NT + j * CT, CT)
                    for i in range(DT, CT):
                        last = nc.scalar.activation(xn[:, b, i, :], t[:, i, :], ACT.Identity, bias=shift[:, b, i:i + 1],
                                                    scale=rstd[:, b, i:i + 1])
                    last.then_inc(e["xn_act_done"], 1)

                def key_high(j, b):
                    s = 2 * j + b
                    act.wait_ge(e["xk_done"], FC * (s + 1))
                    need(act, e["k_done"], 2 * s)
                    nc.scalar.copy(xk_hi[:, :, :], xk[:, :, :]).then_inc(e["xkhi_done"], 1)

                def receptance_high(j, b):
                    s = 2 * j + b
                    act.wait_ge(e["xr_done"], FC * (s + 1))
                    need(act, e["r_done"], s)
                    nc.scalar.copy(xr_hi[:, :, :], xr[:, :, :]).then_inc(e["xrhi_done"], 1)

                def relu(j, b, o):
                    s = 2 * j + b
                    act.wait_ge(e["k_done"], 2 * s + o + 1)
                    need(act, e["kactlo_done"], 2 * s)
                    nc.scalar.activation(relu_k[:, o, :], k_ps[:, o, :], ACT.Relu).then_inc(e["relu_done"], 1)

                def square(j, b, o):
                    act.wait_ge(e["relu_done"], 2 * (2 * j + b) + o + 1)
                    nc.scalar.activation(kact[:, o, :], relu_k[:, o, :], ACT.Square).then_inc(e["kact_done"], 1)

                def square_high(j, b, o):
                    s = 2 * j + b
                    act.wait_ge(e["kact_done"], 2 * s + o + 1)
                    need(act, e["v_done"], 2 * s)
                    nc.scalar.copy(kact_hi[:, o, :], kact[:, o, :]).then_inc(e["kacthi_done"], 1)

                def key_activation(j, b):
                    relu(j, b, 0)
                    square(j, b, 0)
                    relu(j, b, 1)
                    square_high(j, b, 0)
                    square(j, b, 1)
                    square_high(j, b, 1)

                def sigmoid(j, b):
                    s = 2 * j + b
                    act.wait_ge(e["r_done"], s + 1)
                    need(act, e["gated_done"], s)
                    nc.scalar.activation(gate, r_tok, ACT.Sigmoid).then_inc(e["gate_done"], 1)

                def first_block(before_key, after_key):
                    evict_xT(0, 0, True)
                    normalize(0, 1)
                    before_key()
                    key_high(0, 0)
                    after_key()
                    if stage == 1:
                        receptance_high(0, 0)
                        evict_xT(0, 1, True)
                        load_table(ACT.Sigmoid)
                    else:
                        evict_xT(0, 1, True)
                        receptance_high(0, 0)

                def body(j, has):
                    for b in range(2):
                        first = not has(b, -1)
                        if has(b, 2) and not first:
                            normalize(j + 1, b)
                        key_activation(j, b)
                        if first:
                            normalize(1, 0)
                        if has(b, 1):
                            key_high(*at(j, b, 1))
                            receptance_high(*at(j, b, 1))
                        sigmoid(j, b)
                        if has(b, 2):
                            evict_xT(j + 1, b, False)

                def steps():
                    rounds(act, NJ, 1, 2, body)

                return normalize, first_block, steps

            def mem():
                def std(r, q, lo, hi):
                    act.wait_ge(m["var_done"], r + 1)
                    nc.scalar.activation(n_std[:, q, lo:hi], n_var[:, q, lo:hi], ACT.Sqrt).then_inc(m["std_done"], 1)

                def normalize(j, b):
                    s = 2 * j + b
                    act.wait_ge(m["scales_done"], s + 1)
                    need(act, m["T_done"], s)
                    t = tiles(b * NT + j * 2, 2)
                    for i in range(2):
                        last = nc.scalar.activation(m_xn[:, i, :], t[:, i, :], ACT.Identity, bias=n_shift[:, b, 2 + i:3 + i],
                                                    scale=n_rstd[:, b, 2 + i:3 + i])
                    last.then_inc(m["xn_done"], 1)

                def add_normalized(j, b):
                    t = tiles(b * NT + j * 2, 2)
                    for i in range(2):
                        last = nc.scalar.activation(t[:, i, :], t[:, i, :], ACT.Identity, bias=n_shift[:, b, 2 + i:3 + i],
                                                    scale=n_gain[:, b, i:i + 1])
                    last.then_inc(m["res_done"], 1)

                def evict_xT(j, b):
                    s = 2 * j + b
                    act.wait_ge(m["T_done"], s + 1)
                    need(act, m["V_done"], s)
                    nc.scalar.copy(m_xnT[:, :, :], t_bank).then_inc(m["xnT_done"], 1)

                def key_square(j, b):
                    s = 2 * j + b
                    act.wait_ge(m["K_done"], s + 1)
                    need(act, m["ksum_done"], s)
                    nc.scalar.activation(ksq[:, :, :], keys, ACT.Square).then_inc(m["ksq_done"], 1)

                def key_norm(j, b):
                    s = 2 * j + b
                    act.wait_ge(m["ksum_done"], s + 1)
                    need(act, m["kinv_done"], s)
                    nc.scalar.activation(knorm[:, :, :], ksum[:, :, 0:Q], ACT.Sqrt).then_inc(m["knorm_done"], 1)

                def ret_normalize(j, b):
                    s = 2 * j + b
                    act.wait_ge(m["scales_done"], s + 5)
                    need(act, m["nT_done"], s)
                    for i in range(2):
                        last = nc.scalar.activation(normed[:, i, :], ret[:, b, i, :], ACT.Identity, bias=n_shift[:, b, i:i + 1],
                                                    scale=n_rstd[:, b, i:i + 1])
                    last.then_inc(m["normed_done"], 1)

                def store_x(j, b):
                    act.wait_ge(m["O_done"], 2 * j + b + 1)
                    nc.scalar.copy(tiles(b * NT + j * 2, 2), o_bank).then_inc(m["x_done"], 1)

                def evict_nT(j, b):
                    s = 2 * j + b
                    act.wait_ge(m["nT_done"], s + 1)
                    need(act, m["O_done"], s)
                    nc.scalar.copy(normedT[:, :, :], rt_bank).then_inc(m["normedT_done"], 1)

                def first_keys():
                    load_table(ACT.Sqrt)
                    std(0, 0, 2, 4)
                    normalize(0, 0)
                    evict_xT(0, 0)
                    add_normalized(0, 0)
                    std(1, 1, 2, 4)
                    normalize(0, 1)
                    std(2, 0, 2, 4)
                    key_square(0, 0)
                    evict_xT(0, 1)
                    key_norm(0, 0)
                    add_normalized(0, 1)
                    key_square(0, 1)
                    key_norm(0, 1)
                    normalize(1, 0)

                def body(j, has):
                    for b in range(2):
                        ahead, behind = has(b, 2), has(b, -2)
                        if behind:
                            ret_normalize(j - 1, b)
                        if ahead:
                            evict_xT(j + 1, b)
                        if behind:
                            evict_nT(j - 1, b)
                        if has(b, -3):
                            store_x(*at(j, b, -3))
                        if ahead:
                            add_normalized(j + 1, b)
                            key_square(j + 1, b)
                        std(2 * j + b + 3, 1 - b, 0 if has(b, -1) else 2, 4 if has(b, 3) else 2)
                        if ahead:
                            key_norm(j + 1, b)
                        if has(b, 3):
                            normalize(*at(j, b, 3))

                def steps():
                    rounds(act, NP, 2, 2, body)

                def last_but_one():
                    store_x(NP - 2, 1)
                    evict_nT(NP - 1, 0)

                def last_layernorm():
                    std(MS + 3, 1, 0, 2)
                    ret_normalize(NP - 1, 1)
                    store_x(NP - 1, 0)
                    evict_nT(NP - 1, 1)

                def last_store():
                    store_x(NP - 1, 1)

                return first_keys, ret_normalize, steps, last_but_one, last_layernorm, last_store

            act.wait_ge(consts_pool, POOL_CONSTS)
            load_table(ACT.Sigmoid)
            normalize, first_block, ffn_steps = ffn(0)
            first_keys, ret_normalize, mem_steps, last_but_one, last_layernorm, last_store = mem()
            normalize(0, 0)
            first_block(lambda: None, lambda: None)
            act.wait_ge(bias_rows_ready, 1)
            nc.scalar.copy(bias3[:, :], v_flat[:, 0:3 * D]).then_inc(bias_rows_ready, 1)
            ffn_steps()
            first_keys()
            mem_steps()
            normalize, first_block, ffn_steps = ffn(1)
            normalize(0, 0)
            ret_normalize(NP - 1, 0)
            act.wait_ge(shift_zeroed, 1)
            first_block(last_but_one, last_layernorm)
            last_store()
            ffn_steps()

        @block.gpsimd
        def _(pool):
            def prepare():
                nc.gpsimd.memset(ident[:, :], 0.0)
                nc.gpsimd.memset(upto[:, :], 1.0)
                nc.gpsimd.memset(after[:, :], 1.0)
                nc.gpsimd.memset(zeros[:, :], 0.0)
                nc.gpsimd.memset(bias_lines[:, :, :], 0.0)
                nc.gpsimd.memset(xnT[:, :, :, 0:1], 0.0)
                nc.gpsimd.memset(minus_half[:, :], -0.5)
                nc.gpsimd.memset(eps_tile[:, :], LN_EPS)
                nc.gpsimd.iota(pos[:, :], pattern=[[P, NT]], base=1, channel_multiplier=1).then_inc(consts_pool, 1)
                pool.wait_ge(consts_pool, 1)
                nc.gpsimd.affine_select(out=ident[:, :], in_=ident[:, :], compare_op=ALU.not_equal, fill=1.0,
                                        base=0, pattern=[[-1, P]], channel_multiplier=1)
                nc.gpsimd.affine_select(out=upto[:, :], in_=upto[:, :], compare_op=ALU.is_ge, fill=0.0,
                                        base=0, pattern=[[1, P]], channel_multiplier=-1)
                nc.gpsimd.affine_select(out=after[:, :], in_=after[:, :], compare_op=ALU.is_gt, fill=0.0,
                                        base=0, pattern=[[-1, P]], channel_multiplier=1).then_inc(consts_pool, 1)

            prepare()

            def ffn(stage):
                e = ffn_sems[stage]
                xT_ps = transpose_banks[stage]
                r_tok = receptance_banks[stage].rearrange("p h (t n) -> p (h t) n", n=D)

                def inverse_std(j, b):
                    s = 2 * j + b
                    pool.wait_ge(e["stats_done"], s + 1)
                    nc.gpsimd.tensor_tensor(rstd[:, b, :], mv[:, b, :, 1], eps_tile[:, :], ALU.add).then_inc(e["var_done"], 1)
                    pool.wait_ge(e["var_done"], s + 1)
                    nc.gpsimd.tensor_tensor(rstd[:, b, :], rstd[:, b, :], minus_half[:, :], ALU.pow).then_inc(e["rstd_done"], 1)

                def receptance_low(j, b):
                    s = 2 * j + b
                    pool.wait_ge(e["xrhi_done"], s + 1)
                    nc.gpsimd.tensor_tensor(xr_lo[:, :, :], xr[:, :, :], xr_hi[:, :, :].bitcast(F32),
                                            ALU.subtract).then_inc(e["xrlo_done"], 1)

                def residual(j, b):
                    s = 2 * j + b
                    pool.wait_ge(e["gated_done"], s + 1)
                    t = tiles(b * NT + j * CT, CT)
                    nc.gpsimd.tensor_tensor(t, t, gated, ALU.add).then_inc(e["res_done"], 1)

                def first_block():
                    receptance_low(0, 0)
                    inverse_std(1, 0)

                def body(j, has):
                    for b in range(2):
                        if has(b, 3):
                            inverse_std(*at(j, b, 3))
                        if has(b, -1):
                            residual(*at(j, b, -1))
                        if has(b, 1):
                            key_low(pool, nc.gpsimd, e, *at(j, b, 1))
                            receptance_low(*at(j, b, 1))

                def steps():
                    rounds(pool, NJ, 1, 2, body)
                    if stage == 0:
                        residual(NJ - 1, 1)

                return inverse_std, first_block, steps

            def mem():
                def key_sum(j, b):
                    s = 2 * j + b
                    pool.wait_ge(m["ksq_done"], s + 1)
                    need(pool, m["knorm_done"], s)
                    nc.gpsimd.tensor_tensor(ksum[:, :, :], ksq[:, :, 0:2 * Q], ksq[:, :, 2 * Q:4 * Q], ALU.add).then_inc(m["khalf_done"], 1)
                    pool.wait_ge(m["khalf_done"], s + 1)
                    nc.gpsimd.tensor_tensor(ksum[:, :, 0:Q], ksum[:, :, 0:Q], ksum[:, :, Q:2 * Q], ALU.add).then_inc(m["ksum_done"], 1)

                pool.wait_ge(ffn_sems[0]["xr_done"], FC * NS)
                nc.gpsimd.memset(xnT[:, :, :, 0:1], 0.0).then_inc(shift_zeroed, 1)
                key_sum(0, 0)
                bind_sum(nc.gpsimd, 0, 0, 0)
                key_sum(0, 1)
                bind_sum(nc.gpsimd, 0, 0, 1)

                def body(j, has):
                    for b in range(2):
                        if has(b, -1):
                            ret_sum(nc.gpsimd, *at(j, b, -1), 1)
                        if has(b, 1):
                            bind_sum(nc.gpsimd, *at(j, b, 1), 0)
                        if has(b, 2):
                            key_sum(j + 1, b)
                        if has(b, 1):
                            bind_sum(nc.gpsimd, *at(j, b, 1), 1)

                rounds(pool, NP, 2, 2, body)

            inverse_std, first_block, ffn_steps = ffn(0)
            inverse_std(0, 0)
            inverse_std(0, 1)
            first_block()
            ffn_steps()
            mem()
            inverse_std, first_block, ffn_steps = ffn(1)
            inverse_std(0, 0)
            inverse_std(0, 1)
            ret_sum(nc.gpsimd, NP - 1, 1, 1)
            first_block()
            ffn_steps()

        @block.tensor
        def _(pe):
            def fold_bias():
                pe.wait_ge(consts_in, 16 * 4)
                pe.wait_ge(wo_in, 16)
                for o in range(FC):
                    for f in range(FC):
                        last = nc.tensor.matmul(v_ps[:, 0, o:o + 1], wo[:, f, o * P:(o + 1) * P], lnb[:, f:f + 1],
                                                start=f == 0, stop=f == FC - 1)
                last.then_inc(lnb_folded, 1)

            def bias_rows():
                pe.wait_ge(bias_lines_ready, 1)
                for c in range(3 * FC):
                    last = nc.tensor.transpose(v_flat[:, c * P:(c + 1) * P], bias_lines[:, c, :], ident[:, :])
                last.then_inc(bias_rows_ready, 1)

            def parts(out_ap, high, low, f_high, f_low):
                n = 3 * FC
                k = 0
                for f in range(FC):
                    for w, v in ((high, f_high), (low, f_high), (high, f_low)):
                        last = nc.tensor.matmul(out_ap, w(f), v(f), start=k == 0, stop=k == n - 1)
                        k += 1
                return last

            def ffn(stage):
                e = ffn_sems[stage]
                xT_ps = transpose_banks[stage]
                r_tok = receptance_banks[stage].rearrange("p h (t n) -> p (h t) n", n=D)

                def transposes(j, b):
                    s = 2 * j + b
                    pe.wait_ge(e["xn_done"], s + 1)
                    pe.wait_ge(e["xn_act_done"], s + 1)
                    need(pe, e["xnT_done"], s)
                    for f in range(FC):
                        for i in range(CT):
                            last = nc.tensor.transpose(xT_ps[:, f, i * P:(i + 1) * P], xn[:, b, i, f * P:(f + 1) * P], ident[:, :])
                    last.then_inc(e["T_done"], 1)

                def key(j, b):
                    s = 2 * j + b
                    pe.wait_ge(e["xklo_done"], s + 1)
                    need(pe, e["relu_done"], 2 * s)
                    for o in range(FC):
                        parts(k_ps[:, o, :],
                              lambda f: wffn_hi[:, 0, f, o * P:(o + 1) * P], lambda f: wffn_lo[:, 0, f, o * P:(o + 1) * P],
                              lambda f: xk_hi[:, f, :], lambda f: xk_lo[:, f, :]).then_inc(e["k_done"], 1)

                def by_token(dst, x_hi, x_lo, w, first=0, end=CT):
                    for i in range(first, end):
                        last = parts(dst[:, i, :],
                                     lambda f: x_hi[:, f, i * P:(i + 1) * P], lambda f: x_lo[:, f, i * P:(i + 1) * P],
                                     lambda f: wffn_hi[:, w, f, :], lambda f: wffn_lo[:, w, f, :])
                    return last

                def receptance(j, b):
                    s = 2 * j + b
                    pe.wait_ge(e["xrlo_done"], s + 1)
                    need(pe, e["gate_done"], s)
                    by_token(r_tok, xr_hi, xr_lo, 1).then_inc(e["r_done"], 1)

                def value(j, b):
                    s = 2 * j + b
                    pe.wait_ge(e["kactlo_done"], 2 * s + 2)
                    need(pe, e["gated_done"], s)
                    by_token(v_tok, kact_hi, kact_lo, 2, 0, CT // 2).then_inc(e["v_done"], 1)
                    by_token(v_tok, kact_hi, kact_lo, 2, CT // 2, CT).then_inc(e["v_done"], 1)

                def body(j, has):
                    for b in range(2):
                        first = not has(b, -1)
                        key(j, b)
                        if stage == 0 and first:
                            pe.wait_ge(weights_ready, 2)
                        if stage == 1 and first:
                            pe.wait_ge(m["x_done"], MS)
                        receptance(j, b)
                        if has(b, 2):
                            transposes(j + 1, b)
                        if stage == 0 and first:
                            pe.wait_ge(bias_rows_ready, 2)
                        value(j, b)

                def steps():
                    rounds(pe, NJ, 1, 2, body)

                return transposes, steps

            def mem(ffn_transposes):
                def transposes(j, b):
                    s = 2 * j + b
                    pe.wait_ge(m["xn_done"], s + 1)
                    need(pe, m["xnT_done"], s)
                    for f in range(FC):
                        for i in range(2):
                            last = nc.tensor.transpose(t_bank[:, f, i * P:(i + 1) * P], m_xn[:, i, f * P:(f + 1) * P], ident[:, :])
                    last.then_inc(m["T_done"], 1)

                def project(dst, col, done):
                    for i in range(2):
                        for f in range(FC):
                            nc.tensor.matmul(dst[:, i, :], m_xnT[:, f, i * P:(i + 1) * P], wkv[:, f, col:col + D],
                                             start=f == 0, stop=False)
                        last = nc.tensor.matmul(dst[:, i, :], ones[:, :], bias3[:, col:col + D], start=False, stop=True)
                    last.then_inc(done, 1)

                def project_keys(j, b):
                    s = 2 * j + b
                    pe.wait_ge(m["xnT_done"], s + 1)
                    need(pe, m["khat_done"], s)
                    project(keys, 0, m["K_done"])

                def project_values(j, b):
                    s = 2 * j + b
                    need(pe, bprod_done[1], s - 1)
                    project(values[b], D, m["V_done"])

                def sum_upto(j, b, i):
                    s = 2 * j + b
                    pe.wait_ge(bound_done[i], s + 1)
                    nc.tensor.matmul(memory[b], upto[:, :], bound[:, b, i, :], start=False, stop=True,
                                     skip_group_check=True).then_inc(upto_done[i], 1)

                def sum_after(j, b, i):
                    s = 2 * j + b
                    pe.wait_ge(rprod_done[i], s + 1)
                    nc.tensor.matmul(memory[b], after[:, :], bound[:, b, i, :], start=False, stop=True,
                                     skip_group_check=True).then_inc(after_done[i], 1)

                def ret_transposes(j, b):
                    s = 2 * j + b
                    pe.wait_ge(m["normed_done"], s + 1)
                    need(pe, m["normedT_done"], s)
                    for f in range(FC):
                        for i in range(2):
                            last = nc.tensor.transpose(rt_bank[:, f, i * P:(i + 1) * P], normed[:, i, f * P:(f + 1) * P], ident[:, :])
                    last.then_inc(m["nT_done"], 1)

                def output(j, b):
                    s = 2 * j + b
                    pe.wait_ge(m["normedT_done"], s + 1)
                    pe.wait_ge(m["res_done"], s + 1)
                    t = tiles(b * NT + j * 2, 2)
                    need(pe, m["x_done"], s)
                    for i in range(2):
                        for f in range(FC):
                            nc.tensor.matmul(o_bank[:, i, :], normedT[:, f, i * P:(i + 1) * P], wo[:, f, :],
                                             start=f == 0, stop=False)
                        nc.tensor.matmul(o_bank[:, i, :], ones[:, :], bias3[:, 2 * D:], start=False, stop=False)
                        last = nc.tensor.matmul(o_bank[:, i, :], ident[:, :], t[:, i, :], start=False, stop=True)
                    last.then_inc(m["O_done"], 1)

                pe.wait_ge(wkv_in, 16)
                pe.wait_ge(mem_ready, 1)
                pe.wait_ge(ffn_sems[0]["relu_done"], FC * NS)
                for b in range(2):
                    transposes(0, b)
                    project_keys(0, b)
                    if b == 0:
                        pe.wait_ge(ffn_sems[0]["gate_done"], NS)
                    project_values(0, b)
                pe.wait_ge(ffn_sems[0]["gated_done"], NS)
                for b in range(2):
                    nc.tensor.matmul(memory[b], upto[:, :], zeros[:, :], start=True, stop=True, skip_group_check=True)

                def body(j, has):
                    for b in range(2):
                        sum_upto(j, b, 0)
                        if has(b, -1):
                            sum_after(*at(j, b, -1), 1)
                        if has(b, 2):
                            transposes(j + 1, b)
                        if has(b, -2):
                            ret_transposes(j - 1, b)
                        if has(b, 2):
                            project_keys(j + 1, b)
                        sum_after(j, b, 0)
                        sum_upto(j, b, 1)
                        if has(b, 2):
                            project_values(j + 1, b)
                        if not has(b, 1):
                            ffn_transposes(0, 0)
                        if has(b, -2):
                            output(j - 1, b)

                rounds(pe, NP, 2, 2, body)
                ret_transposes(NP - 1, 0)
                output(NP - 1, 0)
                ffn_transposes(0, 1)
                ret_transposes(NP - 1, 1)
                output(NP - 1, 1)

            transposes, ffn_steps = ffn(0)
            pe.wait_ge(consts_pool, POOL_CONSTS)
            transposes(0, 0)
            fold_bias()
            transposes(0, 1)
            bias_rows()
            pe.wait_ge(weights_ready, 1)
            ffn_steps()
            transposes, ffn_steps = ffn(1)
            mem(transposes)
            ffn_steps()


POOL_CONSTS = 2


def kernel(L0_attn_x, L0_attn_Wk, L0_attn_bk, L0_attn_Wv, L0_attn_bv, L0_attn_ln_g, L0_attn_ln_b, L0_attn_Wo, L0_attn_bo,
           L0_ffn_W_r, L0_ffn_W_k, L0_ffn_W_v, L0_ffn_mu_r, L0_ffn_mu_k):
    import numpy as np
    import concourse.bacc as bacc
    from concourse.bass_utils import run_bass_kernel_spmd

    def by_component(a):
        a = np.asarray(a)
        return a.reshape(a.shape[0] // 4, 4, -1).transpose(1, 0, 2).reshape(a.shape)

    arrays = {
        "x": np.asarray(L0_attn_x),
        "w_kv": np.concatenate([by_component(L0_attn_Wk).T, by_component(L0_attn_Wv).T], axis=1),
        "w_o": by_component(np.asarray(L0_attn_Wo).T),
        "w_r": np.asarray(L0_ffn_W_r).T,
        "w_k": np.asarray(L0_ffn_W_k).T,
        "w_v": np.asarray(L0_ffn_W_v).T,
        "columns": np.concatenate([v.reshape(-1, P).T for v in (np.asarray(L0_ffn_mu_r), np.asarray(L0_ffn_mu_k),
                                                                by_component(L0_attn_ln_g), by_component(L0_attn_ln_b),
                                                                by_component(L0_attn_bk), by_component(L0_attn_bv),
                                                                np.asarray(L0_attn_bo))], axis=1),
    }
    arrays = {name: np.ascontiguousarray(a) for name, a in arrays.items()}
    nc = bacc.Bacc("TRN2", target_bir_lowering=False, num_devices=1)
    args = [nc.dram_tensor(name, a.shape, mybir.dt.from_np(a.dtype), kind="ExternalInput").ap() for name, a in arrays.items()]
    out = nc.dram_tensor("out", arrays["x"].shape, F32, kind="ExternalOutput").ap()
    macaron(nc, *args, out)
    r = run_bass_kernel_spmd(nc, [arrays], core_ids=[0])
    return r.results[0]["out"]
```
